# Optimizing a Trainium2 kernel written in Bass

```python
import numpy as np
import jax
import jax.numpy as jnp

def _softmax(x, axis=-1):
    return jax.nn.softmax(x, axis=axis)

def _gelu(x):
    return jax.nn.gelu(x, approximate=True)

def _silu(x):
    return jax.nn.silu(x)

def _sigmoid(x):
    return jax.nn.sigmoid(x)

def _layernorm(x, axis=-1, eps=1e-05):
    m = jnp.mean(x, axis=axis, keepdims=True)
    v = jnp.var(x, axis=axis, keepdims=True)
    return (x - m) / jnp.sqrt(v + eps)

def _scatter_add(tgt, idx, src, axis=0):
    return tgt.at[idx].add(src)

def _segment_sum(src, seg, n):
    return jax.ops.segment_sum(src, seg, n)
kernel_name = 'mk_gnn_ffn_d1_gnn_r32_bfd571'

def setup_inputs(seed: int=0):
    np.random.seed(seed)
    _w = jnp.asarray

    def _rec_inputs():
        import jax
        import jax.numpy as jnp
        _gk = jax.random.key(seed)
        x = -0.0003713 + 1 * jax.random.normal(jax.random.fold_in(_gk, 1), (3125, 256), jnp.float32)
        src = jax.random.randint(jax.random.fold_in(_gk, 2), (50000,), 0, 3125, jnp.int32)
        dst = jnp.minimum((3125 * jax.random.uniform(jax.random.fold_in(_gk, 3), (50000,)) ** 2.0).astype(jnp.int32), 99999)
        _o = jnp.argsort(dst, stable=True)
        src = src[_o]
        dst = dst[_o]
        edge_attr_32 = 0.000189758 + 1.00013 * jax.random.normal(jax.random.fold_in(_gk, 11), (50000, 32), jnp.float32)
        return (x, src, dst, edge_attr_32)
    x, src, dst, edge_attr_32 = _rec_inputs()

    def _L0_gnn_setup():
        import jax, jax.numpy as jnp
        import numpy as np
        N_NODES = 50000
        N_EDGES = 50000
        IN_CH = 256
        ADAPTER = 64
        EDGE_DIM = 32
        key = jax.random.key(seed)
        ks = jax.random.split(key, 12)
        s = lambda k, shape: jax.random.normal(k, shape, dtype=jnp.float32) * 0.05
        x = jax.random.normal(ks[0], (N_NODES, IN_CH), dtype=jnp.float32)
        edge_index = jax.random.randint(ks[1], (2, N_EDGES), 0, N_NODES, dtype=jnp.int64)
        edge_attr = jax.random.normal(ks[2], (N_EDGES, EDGE_DIM), dtype=jnp.float32)
        return {'x': x, 'edge_index': edge_index, 'edge_attr': edge_attr, 'W_down': s(ks[3], (ADAPTER, IN_CH)), 'b_down': jnp.zeros((ADAPTER,), jnp.float32), 'W_time': s(ks[4], (ADAPTER, EDGE_DIM)), 'b_time': jnp.zeros((ADAPTER,), jnp.float32), 'W_fusion': s(ks[5], (ADAPTER, 2 * ADAPTER)), 'b_fusion': jnp.zeros((ADAPTER,), jnp.float32), 'W_up': s(ks[6], (IN_CH, ADAPTER)), 'b_up': jnp.zeros((IN_CH,), jnp.float32)}
    _L0_gnn_all = _L0_gnn_setup()
    _L0_gnn_in = {k: v for k, v in _L0_gnn_all.items() if k in ('W_down', 'b_down', 'W_time', 'b_time', 'W_fusion', 'b_fusion', 'W_up', 'b_up')}
    del _L0_gnn_all

    def _L0_ffn_setup():
        import jax, jax.numpy as jnp
        import numpy as np
        B, K, D = (512, 16, 256)
        E = 32
        H = int(D * 0.25)
        key = jax.random.key(seed)
        ks = jax.random.split(key, 7)
        d_rs = D ** (-0.5)
        h_rs = H ** (-0.5)
        x = jax.random.normal(ks[0], (B, K, D), dtype=jnp.float32)
        router_w = jax.random.uniform(ks[1], (E, D), jnp.float32, -d_rs, d_rs)
        router_b = jax.random.uniform(ks[2], (E,), jnp.float32, -d_rs, d_rs)
        W1 = jax.random.uniform(ks[3], (E, D, H), jnp.float32, -h_rs, h_rs)
        b1 = jax.random.uniform(ks[4], (E, H), jnp.float32, -h_rs, h_rs)
        W2 = jax.random.uniform(ks[5], (E, H, D), jnp.float32, -d_rs, d_rs)
        b2 = jax.random.uniform(ks[6], (E, D), jnp.float32, -d_rs, d_rs)
        return {'x': x, 'router_w': router_w, 'router_b': router_b, 'W1': W1, 'b1': b1, 'W2': W2, 'b2': b2}
    _L0_ffn_all = _L0_ffn_setup()
    _L0_ffn_in = {k: v for k, v in _L0_ffn_all.items() if k in ('router_w', 'router_b', 'W1', 'b1', 'W2', 'b2')}
    del _L0_ffn_all
    return {'x': x, 'src': src, 'dst': dst, 'edge_attr_32': edge_attr_32, 'L0_gnn_W_down': _L0_gnn_in['W_down'], 'L0_gnn_b_down': _L0_gnn_in['b_down'], 'L0_gnn_W_time': _L0_gnn_in['W_time'], 'L0_gnn_b_time': _L0_gnn_in['b_time'], 'L0_gnn_W_fusion': _L0_gnn_in['W_fusion'], 'L0_gnn_b_fusion': _L0_gnn_in['b_fusion'], 'L0_gnn_W_up': _L0_gnn_in['W_up'], 'L0_gnn_b_up': _L0_gnn_in['b_up'], 'L0_ffn_router_w': _L0_ffn_in['router_w'], 'L0_ffn_router_b': _L0_ffn_in['router_b'], 'L0_ffn_W1': _L0_ffn_in['W1'], 'L0_ffn_b1': _L0_ffn_in['b1'], 'L0_ffn_W2': _L0_ffn_in['W2'], 'L0_ffn_b2': _L0_ffn_in['b2']}

def reference(x, src, dst, edge_attr_32, L0_gnn_W_down, L0_gnn_b_down, L0_gnn_W_time, L0_gnn_b_time, L0_gnn_W_fusion, L0_gnn_b_fusion, L0_gnn_W_up, L0_gnn_b_up, L0_ffn_router_w, L0_ffn_router_b, L0_ffn_W1, L0_ffn_b1, L0_ffn_W2, L0_ffn_b2):
    import jax
    import jax.numpy as jnp

    def _L0_gnn_ref(x, edge_index, edge_attr, W_down, b_down, W_time, b_time, W_fusion, b_fusion, W_up, b_up):
        import jax, jax.numpy as jnp
        import numpy as np
        N_NODES = 50000
        N_EDGES = 50000
        IN_CH = 256
        ADAPTER = 64
        EDGE_DIM = 32
        n = x.shape[0]
        node_feat = jax.nn.relu(x @ W_down.T + b_down)
        time_feat = jax.nn.relu(edge_attr @ W_time.T + b_time)
        src = edge_index[0]
        sums = jax.ops.segment_sum(time_feat, src, num_segments=n)
        counts = jax.ops.segment_sum(jnp.ones((time_feat.shape[0],), jnp.float32), src, num_segments=n)
        node_time_feat = sums / jnp.maximum(counts, 1.0)[:, None]
        combined = jnp.concatenate([node_feat, node_time_feat], axis=-1)
        fused = jax.nn.relu(combined @ W_fusion.T + b_fusion)
        out = fused @ W_up.T + b_up
        return x + out

    def _L0_ffn_ref(x, router_w, router_b, W1, b1, W2, b2):
        import jax, jax.numpy as jnp
        import numpy as np
        B, K, D = (512, 16, 256)
        E = 32
        H = int(D * 0.25)
        xf = x.reshape(-1, D)
        logits = xf @ router_w.T + router_b
        idx = jnp.argmax(logits, axis=-1)
        w1t = jnp.take(W1, idx, axis=0)
        h = jnp.einsum('nd,ndh->nh', xf, w1t) + jnp.take(b1, idx, axis=0)
        h = jax.nn.relu(h)
        w2t = jnp.take(W2, idx, axis=0)
        out = jnp.einsum('nh,nhd->nd', h, w2t) + jnp.take(b2, idx, axis=0)
        out = jax.nn.relu(out)
        return out.reshape(x.shape)
    edge_index = jnp.stack([src, dst])
    x = x + _L0_gnn_ref(_layernorm(x, axis=-1), edge_index, edge_attr_32, L0_gnn_W_down, L0_gnn_b_down, L0_gnn_W_time, L0_gnn_b_time, L0_gnn_W_fusion, L0_gnn_b_fusion, L0_gnn_W_up, L0_gnn_b_up)
    x = x + _L0_ffn_ref(_layernorm(x, axis=-1)[None], L0_ffn_router_w, L0_ffn_router_b, L0_ffn_W1, L0_ffn_b1, L0_ffn_W2, L0_ffn_b2)[0]
    return x

_drawn_inputs = setup_inputs


def setup_inputs(seed=0):
    import zlib

    import numpy as np

    out = dict(_drawn_inputs(seed))
    spreads = {'L0_gnn_b_down': (0.0, 0.8),
     'L0_gnn_b_time': (0.0, 2.0),
     'L0_gnn_b_fusion': (0.0, 0.395),
     'L0_gnn_b_up': (0.0, 0.1)}
    factors = {'edge_attr_32': 8.0, 'L0_gnn_W_time': 8.0, 'L0_ffn_b1': 8.0, 'L0_ffn_b2': 4.568}
    for name, (base, spread) in spreads.items():
        noise = np.random.default_rng([zlib.crc32(name.encode()), seed]).standard_normal(out[name].shape)
        drawn = base * np.exp(spread * noise) if base else spread * noise
        out[name] = jnp.asarray(drawn.astype(out[name].dtype))
    for name, factor in factors.items():
        out[name] = (out[name] * factor).astype(out[name].dtype)
    return out
```

```python
from contextlib import ExitStack

import numpy as np
import concourse.bass as bass
from concourse import mybir

P = 128
NODES, CH, EDGES, ED = 3125, 256, 50000, 32
AD = 64
EXPERTS = 32
NB = -(-NODES // P)
CHUNKS, PAIRS, BATCH = 4, 7, 7
CT = PAIRS * 2 * BATCH
ET = CHUNKS * CT
GRP, GRPS = 6, 3
ST = PAIRS * GRPS * GRP
assert ET * P >= EDGES and ST >= CT + NB - 1 and ST <= P
ROW = AD + 2
PER_BANK, SLOT = 7, 72
BANK = 512
XT = NB + EXPERTS - 1
PRE = 5
EPS = 1e-5

f32, bf16, i32, u32 = mybir.dt.float32, mybir.dt.bfloat16, mybir.dt.int32, mybir.dt.uint32
ALU, ACT = mybir.AluOpType, mybir.ActivationFunctionType
AXX = mybir.AxisListType.X
ds = bass.ds


class Count:

    def __init__(self, eng, sem):
        self.eng, self.sem, self.n = eng, sem, 0

    def after(self, ins):
        ins.then_inc(self.sem, 1)
        self.n = self.n + 1
        self.eng.wait_ge(self.sem, self.n)

    def loop(self, i, start, stop, steps, body):
        n0 = self.n
        self.n = n0 + (i - start) * steps
        base = self.n
        body(i)
        self.n = n0 + (stop - start) * steps


def program(nc, x, src, attr_t, wd_t, bd, wt_t, bt, wf_t, bf, wu_t, bu, rw_t, rb, w1, b1, w2, b2, out):
    ctx = ExitStack()
    with ctx:
        def sb(name, shape, dt=f32):
            return ctx.enter_context(nc.sbuf_tensor(name, shape, dt))

        def sem(name):
            return ctx.enter_context(nc.semaphore(name))

        edges_sorted = nc.dram_tensor("edges_sorted", (CHUNKS * P * ST, ROW), f32, kind="Internal").ap()
        tok_sorted = nc.dram_tensor("tok_sorted", (XT * P, CH), f32, kind="Internal").ap()
        tok_out = nc.dram_tensor("tok_out", (XT * P, CH), f32, kind="Internal").ap()

        ident = sb("ident", [P, P])
        ones = sb("ones", [P, P])
        before = sb("before", [P, P])
        iota_i = sb("iota_i", [P, P], i32)
        iota = sb("iota", [P, P])
        part_i = sb("part_i", [P, 1], i32)
        part = sb("part", [P, 1])
        slot_w = sb("slot_w", [P, NB])
        empty_row = sb("empty_row", [P, 18 * ROW])
        zeros = sb("zeros", [P, 2 * CH])
        zrow = zeros[0:1, 0:BANK]
        epsb = sb("epsb", [P, 1])
        chunk_base = sb("chunk_base", [P, CHUNKS])

        src_i = sb("src_i", [P, ET], i32)
        tmp_i = sb("tmp_i", [P, ET], i32)
        blk = sb("blk", [P, ET])
        lo = sb("lo", [P, ET])
        rows_i = sb("rows_i", [P, ET], i32)
        onehot = sb("onehot", [P, NB, CT], bf16)
        cum = sb("cum", [P, NB, CT])
        pos = sb("pos", [P, CT])
        pos_i = sb("pos_i", [P, CT], i32)
        pos_h = sb("pos_h", [P, CT], i32)
        pos_l = sb("pos_l", [P, CT], i32)
        cend = sb("cend", [P, EXPERTS + 1])
        cnt = sb("cnt", [P, EXPERTS])
        nt_i = sb("nt_i", [P, EXPERTS], i32)
        nt = sb("nt", [P, EXPERTS])
        tend = sb("tend", [P, EXPERTS])
        base = sb("base", [P, EXPERTS])
        le = sb("le", [P, EXPERTS])
        off = sb("off", [P, 1])
        table = sb("table", [1, CHUNKS + 1, P], i32)

        attr_sb = sb("attr_sb", [ED + 1, 2, BATCH * P])
        ring = sb("ring", [P, 2, BATCH * ROW])
        idx_ring = sb("idx_ring", [P, 2, BATCH], u32)
        edges_sb = sb("edges_sb", [P, ST * ROW])
        node_oh = sb("node_oh", [P, GRPS, GRP * P])

        wd_sb = sb("wd_sb", [P, 2, AD])
        bd_sb = sb("bd_sb", [AD, 1])
        wt_sb = sb("wt_sb", [ED + 1, AD])
        wf_sb = sb("wf_sb", [AD, 2, 2, AD])
        bf_sb = sb("bf_sb", [AD, 1])
        wu_sb = sb("wu_sb", [AD + 1, CH])
        rw_sb = sb("rw_sb", [P, 2, EXPERTS])
        rb_sb = sb("rb_sb", [1, EXPERTS])
        w1_sb = sb("w1_sb", [P, EXPERTS * 2 * AD])
        w2_sb = sb("w2_sb", [AD + 1, EXPERTS * CH])

        xs = sb("xs", [P, NB, CH])
        x1n = sb("x1n", [P, NB, CH])
        nrm = sb("nrm", [P, PRE, CH])
        flat_n = x1n[:, :, :].rearrange("p b c -> p (b c)")
        tmean = flat_n[:, 0:NB * AD]
        nfT = flat_n[0:AD, NB * AD:NB * (AD + P)]
        stats = sb("stats", [P, PRE, 6])
        mv5 = sb("mv5", [P, PRE, 2])
        mv = sb("mv", [P, NB, 2])
        rstd = sb("rstd", [P, NB])
        rcount = sb("rcount", [P, NB])
        xT = sb("xT", [P, 2, 2 * P])
        fT = sb("fT", [AD + 1, PRE * P])
        top = sb("top", [P, PRE, 8])
        topi = sb("topi", [P, PRE, 8], u32)
        hid = sb("hid", [P, 2, AD])
        oh_flat = node_oh[:, :, :].rearrange("p r n -> p (r n)")
        mean5 = oh_flat[:, 0:PRE * AD]
        meanT = oh_flat[0:AD, PRE * AD:PRE * (AD + P)]
        b1_sb = edges_sb[0:1, 4 * CH:4 * CH + EXPERTS * AD]
        tok_in = edges_sb[:, 0:2 * CH].rearrange("p (h c) -> p h c", h=2)
        tok_res = edges_sb[:, 2 * CH:4 * CH].rearrange("p (h c) -> p h c", h=2)

        sums = ctx.enter_context(nc.psum_tensor("sums", [P, 4 * BANK], f32))
        tfp = ctx.enter_context(nc.psum_tensor("tfp", [P, 2 * BANK], f32))
        trp = ctx.enter_context(nc.psum_tensor("trp", [P, BANK], f32))
        mmp = ctx.enter_context(nc.psum_tensor("mmp", [P, BANK], f32))
        HALF = PRE * P // 2
        fused_p = [mmp[:, 0:HALF], trp[:, 0:HALF]]
        banks = [sums[:, k * BANK:(k + 1) * BANK] for k in range(4)]
        up_p = [banks[r % 4][:, 0:CH] for r in range(PRE)]
        lg_p = [b[:, 0:EXPERTS] for b in (*banks, trp[:, :])]
        rt_p = [tfp[:, h * BANK:h * BANK + 2 * P] for h in range(2)]
        res_p = [banks[h][:, 0:CH] for h in range(2)]
        nf_p = banks[0][0:AD, 0:P]
        slots = sums[:, :].rearrange("p (k c) -> p k c", k=4)
        before_p, total_p, table_p = mmp[:, 0:EXPERTS], mmp[:, 64:64 + EXPERTS], mmp[0:1, 128:256]

        consts = sem("consts")
        ones_set = sem("ones_set")
        src_in, x_in, gw_in, mw_in, late_in = sem("src_in"), sem("x_in"), sem("gw_in"), sem("mw_in"), sem("late_in")
        cleared = sem("cleared")
        tok_cleared = sem("tok_cleared")
        b1_in = sem("b1_in")
        attr_in = [sem(f"attr_in{h}") for h in range(2)]
        tf_done = [sem(f"tf_done{h}") for h in range(2)]
        ring_ready = [sem(f"ring_ready{h}") for h in range(2)]
        scattered = [sem(f"scattered{h}") for h in range(2)]
        edges_in = sem("edges_in")
        oh_ready = [sem(f"oh_ready{r}") for r in range(GRPS)]
        oh_used = [sem(f"oh_used{r}") for r in range(GRPS)]
        dve_step, act_step, pe_step, pool_step = sem("dve_step"), sem("act_step"), sem("pe_step"), sem("pool_step")
        cnt_ready, cnt_sum, off_ready, off_row, table_ready, rows_ready = (
            sem("cnt_ready"), sem("cnt_sum"), sem("off_ready"), sem("off_row"), sem("table_ready"), sem("rows_ready"))
        var_ready, std_ready, xn_ready = sem("var_ready"), sem("std_ready"), sem("xn_ready")
        tr_done, tr_copied, nf_done, nf_ready = sem("tr_done"), sem("tr_copied"), sem("nf_done"), sem("nf_ready")
        mean_ready, mt_done, mt_copied, fu_done, fu_ready, up_done, x1_ready = (
            sem("mean_ready"), sem("mt_done"), sem("mt_copied"), sem("fu_done"), sem("fu_ready"), sem("up_done"), sem("x1_ready"))
        x1n_kept, chosen = sem("x1n_kept"), sem("chosen")
        x1n_ready, rt_done, rt_copied, lg_done, lg_used = (
            sem("x1n_ready"), sem("rt_done"), sem("rt_copied"), sem("lg_done"), sem("lg_used"))
        tok_rows, tok_scat = sem("tok_rows"), sem("tok_scat")
        tok_loaded = [sem(f"tok_loaded{h}") for h in range(2)]
        tok_tr, tok_trc, hid_done, hid_ready, ht_done, ht_ready, o_done, o_ready = (
            sem("tok_tr"), sem("tok_trc"), sem("hid_done"), sem("hid_ready"), sem("ht_done"), sem("ht_ready"),
            sem("o_done"), sem("o_ready"))
        stored = [sem(f"stored{h}") for h in range(2)]
        gathered = [sem(f"gathered{h}") for h in range(5)]
        y_ready = sem("y_ready")
        y_out = sem("y_out")

        from_one = [*ring_ready, *oh_used, tr_copied, nf_ready, tr_done, mt_copied, fu_ready, x1_ready, fu_done, up_done,
                    mt_done, rt_copied, lg_used, rt_done, x1n_kept, o_ready]

        def settled(eng):
            eng.sem_inc(passed[eng.engine], 1)

        passed = {eng.engine: sem(f"passed_{name}") for name, eng in
                  (("dve", nc.vector), ("pool", nc.gpsimd), ("pe", nc.tensor))}
        block = ctx.enter_context(nc.Block())

        @block.sync
        def _(sp):
            sp.dma_start(src_i[:, :], src.rearrange("(p t) -> p t", p=P)).then_inc(src_in, 16)
            sp.wait_ge(consts, 1)
            def clear(c):
                dst = edges_sorted[:, :].rearrange("(c p k j) f -> c p k (j f)", c=CHUNKS, p=P, j=18)
                sp.dma_start(dst[ds(c, 1)].rearrange("o p k n -> (o p) k n"),
                             empty_row[:, :].rearrange("p (o n) -> p o n", o=1).to_broadcast([P, ST // 18, 18 * ROW])
                             ).then_inc(cleared, 16)

            def attributes(q):
                for h in range(2):
                    sp.wait_ge(tf_done[h], q)
                    sp.dma_start(attr_sb[0:ED, h, :], attr_t[:, ds((2 * q + h) * BATCH * P, BATCH * P)]
                                 ).then_inc(attr_in[h], 16)

            clear(0)
            sp.dma_start(wt_sb[0:ED, :], wt_t).then_inc(gw_in, 16)
            sp.dma_start(wt_sb[ED:ED + 1, :], bt).then_inc(gw_in, 16)
            attributes(0)
            sp.dma_start(xs[:, :, :], x.rearrange("(b p) c -> p b c", p=P)).then_inc(x_in, 16)
            sp.dma_start(wd_sb[:, :, :], wd_t.rearrange("(k p) n -> p k n", p=P)).then_inc(mw_in, 16)
            sp.dma_start(bd_sb[:, :], bd).then_inc(mw_in, 16)
            for twice in range(2):
                sp.dma_start(wf_sb[:, :, twice, :], wf_t.rearrange("(k p) n -> p k n", p=AD)).then_inc(late_in, 16)
            sp.dma_start(bf_sb[:, :], bf).then_inc(late_in, 16)
            sp.dma_start(wu_sb[0:AD, :], wu_t).then_inc(late_in, 16)
            sp.dma_start(wu_sb[AD:AD + 1, :], bu).then_inc(late_in, 16)
            sp.dma_start(rw_sb[:, :, :], rw_t.rearrange("(k p) n -> p k n", p=P)).then_inc(late_in, 16)
            sp.dma_start(rb_sb[:, :], rb).then_inc(late_in, 16)
            with sp.Fori(1, PAIRS) as q:
                attributes(q)
            sp.wait_ge(cleared, 16)
            clear(1)
            sp.dma_start(w1_sb[:, :].rearrange("p (e k n) -> p e k n", e=EXPERTS, k=2)[:, :, 0, :],
                         w1[:, 0:P, :].rearrange("e p n -> p e n")).then_inc(late_in, 16)
            sp.dma_start(w1_sb[:, :].rearrange("p (e k n) -> p e k n", e=EXPERTS, k=2)[:, :, 1, :],
                         w1[:, P:CH, :].rearrange("e p n -> p e n")).then_inc(late_in, 16)
            sp.dma_start(w2_sb[0:AD, :].rearrange("p (e n) -> p e n", e=EXPERTS),
                         w2.rearrange("e p n -> p e n")).then_inc(late_in, 16)
            sp.dma_start(w2_sb[AD:AD + 1, :], b2).then_inc(late_in, 16)
            sp.dma_start(tok_sorted[:, :].rearrange("(p k j) c -> p k (j c)", p=P, j=2),
                         zeros[:, :].rearrange("p (o n) -> p o n", o=1).to_broadcast([P, XT // 2, 2 * CH])
                         ).then_inc(tok_cleared, 16)

            def load_sorted(c):
                for h in range(2):
                    sp.wait_ge(scattered[h], BATCH * 16 * PAIRS * (c + 1))
                for r in range(GRPS):
                    sp.wait_ge(oh_used[r], 1 + PAIRS * c)
                sp.dma_start(edges_sb[:, :], edges_sorted[:, :].rearrange("(c p j) f -> c p (j f)", c=CHUNKS, p=P)
                             [ds(c, 1)].rearrange("o p n -> (o p) n")).then_inc(edges_in, 16)

            def stage(s):
                attributes(PAIRS * s)
                load_sorted(s - 1)
                with sp.Fori(1, PAIRS) as i:
                    attributes(PAIRS * s + i)

            with sp.Fori(1, CHUNKS - 1) as s:
                sp.wait_ge(cleared, 16 * s + 16)
                clear(s + 1)
                stage(s)
            stage(CHUNKS - 1)
            load_sorted(CHUNKS - 1)
            for r in range(GRPS):
                sp.wait_ge(oh_used[r], 1 + PAIRS * CHUNKS)
            sp.dma_start(b1_sb, b1).then_inc(b1_in, 16)

            sp.wait_ge(tok_scat, 16 * NB)
            def load_tile(j, h):
                sp.dma_start(tok_in[:, h, :], tok_sorted[ds(j * P, P), :]).then_inc(tok_loaded[h], 16)
            def store_tile(j, h, n):
                sp.wait_ge(o_ready, 1 + n)
                sp.dma_start(tok_out[ds(j * P, P), :], tok_res[:, h, :]).then_inc(stored[h], 16)
            for h in range(2):
                load_tile(h, h)
            with sp.Fori(0, XT // 2 - 1) as m:
                for h in range(2):
                    store_tile(2 * m + h, h, 2 * m + h + 1)
                    sp.wait_ge(tok_tr, 2 * m + h + 1)
                    load_tile(2 * m + h + 2, h)
            for h in range(2):
                store_tile(XT - 2 + h, h, XT - 1 + h)

            for b in range(NB):
                n = min(P, NODES - b * P)
                sp.wait_ge(y_ready, b + 1)
                sp.dma_start(out[b * P:b * P + n, :], xs[0:n, b, :]).then_inc(y_out, 16)
            sp.wait_ge(y_out, 16 * NB)

        @block.gpsimd
        def _(pool):
            for started in from_one:
                pool.sem_inc(started, 1)
            pool.memset(empty_row[:, :].rearrange("p (j f) -> p j f", f=ROW)[:, :, 0:ROW - 1], 0.0).then_inc(pool_step, 1)
            pool.memset(zeros[:, :], 0.0).then_inc(pool_step, 1)
            pool.wait_ge(pool_step, 2)
            pool.memset(empty_row[:, :].rearrange("p (j f) -> p j f", f=ROW)[:, :, ROW - 1:ROW], -1.0).then_inc(consts, 1)
            pool.iota(iota_i[:, :], pattern=[[1, P]], base=0, channel_multiplier=0).then_inc(consts, 1)
            pool.iota(part_i[:, :], pattern=[[1, 1]], base=0, channel_multiplier=1).then_inc(consts, 1)
            pool.memset(ident[:, :], 0.0).then_inc(pool_step, 1)
            pool.memset(before[:, :], 0.0).then_inc(pool_step, 1)
            pool.wait_ge(pool_step, 4)
            pool.affine_select(out=before[:, :], in_=before[:, :], compare_op=ALU.is_ge, fill=1.0,
                               base=0, pattern=[[-1, P]], channel_multiplier=1).then_inc(consts, 1)
            pool.affine_select(out=ident[:, :], in_=ident[:, :], compare_op=ALU.not_equal, fill=1.0,
                               base=0, pattern=[[-1, P]], channel_multiplier=1).then_inc(consts, 1)

            with pool.Fori(0, CHUNKS) as s:
                pool.wait_ge(cleared, 16 * s + 16)
                settled(pool)
                with pool.Fori(0, PAIRS) as i:
                    for h in range(2):
                        pool.wait_ge(ring_ready[h], 1 + 3 * (PAIRS * s + i + 1))
                        settled(pool)
                        for j in range(BATCH):
                            pool.indirect_dma_start(
                                edges_sorted[:, :], bass.IndirectOffsetOnAxis(ap=idx_ring[:, h, j:j + 1], axis=0),
                                ring[:, h, j * ROW:(j + 1) * ROW], None).then_inc(scattered[h], 16)

            with pool.Fori(0, NB // PRE) as g:
                for r in range(PRE):
                    pool.wait_ge(x1n_ready, PRE * g + r + 1)
                    pool.tensor_copy(x1n[:, ds(PRE * g + r, 1), :].rearrange("p o c -> p (o c)"), nrm[:, r, :]
                                     ).then_inc(x1n_kept, 1)
            pool.wait_ge(x1n_kept, 1 + NB)
            pool.wait_ge(tok_cleared, 16)
            pool.wait_ge(tok_rows, 1)
            for b in range(NB):
                pool.indirect_dma_start(tok_sorted[:, :], bass.IndirectOffsetOnAxis(ap=rows_i[:, b:b + 1].bitcast(u32), axis=0),
                                        x1n[:, b, :], None).then_inc(tok_scat, 16)
            for h in range(2):
                pool.wait_ge(stored[h], 16 * (XT // 2))
            pool.wait_ge(tok_scat, 16 * NB)
            for b in range(NB):
                pool.indirect_dma_start(x1n[:, b, :], None, tok_out[:, :],
                                        bass.IndirectOffsetOnAxis(ap=rows_i[:, b:b + 1].bitcast(u32), axis=0)
                                        ).then_inc(gathered[b // 5], 16)

        @block.scalar
        def _(act):
            def batches(q, first=False):
                for h in range(2):
                    act.wait_ge(tf_done[h], q + 1)
                    if not first:
                        act.wait_ge(scattered[h], BATCH * 16 * q)
                    r = ring[:, h, :].rearrange("p (j f) -> p j f", f=ROW)
                    act.activation(r[:, :, 0:AD], tfp[:, h * BANK:h * BANK + BATCH * AD].rearrange("p (j f) -> p j f", f=AD),
                                   ACT.Relu).then_inc(ring_ready[h], 1)
                    act.activation(r[:, :, ROW - 1], lo[:, ds((2 * q + h) * BATCH, BATCH)], ACT.Copy).then_inc(ring_ready[h], 1)
                    act.activation(idx_ring[:, h, :], rows_i[:, ds((2 * q + h) * BATCH, BATCH)], ACT.Copy
                                   ).then_inc(ring_ready[h], 1)

            def stdev(n):
                act.wait_ge(var_ready, NB // PRE * n)
                act.activation(rstd[:, :], mv[:, :, 1], ACT.Sqrt, bias=epsb[:, 0:1]).then_inc(std_ready, 1)

            def prepare(b):
                act.wait_ge(tr_done, 1 + b + 1)
                act.activation(xT[:, 0, :], trp[:, 0:2 * P], ACT.Copy).then_inc(tr_copied, 1)
                act.wait_ge(nf_done, b + 1)
                act.activation(nfT[:, ds(b * P, P)], nf_p, ACT.Relu, bias=bd_sb[:, 0:1]).then_inc(nf_ready, 1)

            act.wait_ge(ones_set, 1)
            stdev(1)
            act.wait_ge(mw_in, 32)
            act.wait_ge(rows_ready, 1)
            batches(0, first=True)
            for r in range(PRE):
                prepare(r)
            with act.Fori(1, NB // PRE) as i:
                batches(i)
                for r in range(PRE):
                    prepare(i * PRE + r)
            with act.Fori(NB // PRE, PAIRS) as i:
                batches(i)
            with act.Fori(1, CHUNKS) as s:
                act.wait_ge(rows_ready, s + 1)
                with act.Fori(0, PAIRS) as i:
                    batches(PAIRS * s + i)

            act.wait_ge(late_in, 16 * 11)
            with act.Fori(0, NB // PRE) as g:
                act.wait_ge(mt_done, 1 + g + 1)
                act.wait_ge(fu_done, 1 + g)
                act.activation(meanT[:, 0:4 * P], tfp[0:AD, 0:4 * P], ACT.Copy).then_inc(mt_copied, 1)
                act.activation(meanT[:, 4 * P:5 * P], tfp[0:AD, 4 * P:5 * P], ACT.Copy).then_inc(mt_copied, 1)
                act.wait_ge(fu_done, 1 + g + 1)
                act.wait_ge(up_done, 1 + PRE * g)
                for k, half in enumerate(fused_p):
                    act.activation(fT[0:AD, k * HALF:(k + 1) * HALF], half[0:AD], ACT.Relu, bias=bf_sb[:, 0:1]).then_inc(fu_ready, 1)
            stdev(2)
            with act.Fori(0, NB // PRE) as g:
                for r in range(PRE):
                    act.wait_ge(rt_done, 1 + PRE * g + r + 1)
                    act.activation(xT[:, r % 2, :], rt_p[r % 2], ACT.Copy).then_inc(rt_copied, 1)
            with act.Fori(0, XT) as j:
                act.wait_ge(tok_tr, j + 1)
                act.activation(xT[:, 0, :], trp[:, 0:2 * P], ACT.Copy).then_inc(tok_trc, 1)
                act.wait_ge(hid_done, j + 1)
                act.activation(hid[:, 0, :], mmp[:, 0:AD], ACT.Relu).then_inc(hid_ready, 1)
                act.wait_ge(ht_done, j + 1)
                act.activation(fT[0:AD, 0:P], trp[0:AD, 256:256 + P], ACT.Copy).then_inc(ht_ready, 1)

        @block.vector
        def _(dve):
            st = Count(dve, dve_step)
            V = nc.vector
            dve.wait_ge(consts, 3)
            V.memset(ones[:, :], 1.0).then_inc(dve_step, 1)
            V.memset(attr_sb[ED:ED + 1, :, :], 1.0).then_inc(dve_step, 1)
            V.memset(ring[:, :, :].rearrange("p h (j f) -> p h j f", f=ROW)[:, :, :, AD], 1.0).then_inc(dve_step, 1)
            V.memset(fT[AD:AD + 1, :], 1.0).then_inc(dve_step, 1)
            V.memset(epsb[:, :], EPS).then_inc(dve_step, 1)
            V.memset(cend[:, 0:1], 0.0).then_inc(dve_step, 1)
            V.memset(slot_w[:, :], float(SLOT)).then_inc(dve_step, 1)
            V.tensor_copy(iota[:, :], iota_i[:, :]).then_inc(dve_step, 1)
            V.tensor_copy(part[:, :], part_i[:, :]).then_inc(dve_step, 1)
            st.n = 9
            dve.wait_ge(dve_step, st.n)
            V.memset(slot_w[:, PER_BANK - 1:NB:PER_BANK], float(BANK - (PER_BANK - 1) * SLOT)).then_inc(ones_set, 1)
            dve.wait_ge(ones_set, 1)
            dve.wait_ge(src_in, 16)
            st.after(V.tensor_scalar(tmp_i[:, :], src_i[:, :], 7, None, ALU.logical_shift_right))
            st.after(V.tensor_copy(blk[:, :], tmp_i[:, :]))
            st.after(V.tensor_scalar(tmp_i[:, :], src_i[:, :], P - 1, None, ALU.bitwise_and))
            st.after(V.tensor_copy(lo[:, :], tmp_i[:, :]))

            def rank(key, n, w, c, row_of, weight, last, rows_out, table_out):
                oh = onehot[:, :, :].rearrange("p b t -> p (b t)")[:, 0:w * n].rearrange("p (b t) -> p b t", t=n)
                cu = cum[:, :, :].rearrange("p b t -> p (b t)")[:, 0:w * n].rearrange("p (b t) -> p b t", t=n)
                flat = lambda a: a.rearrange("p b t -> p (b t)")
                st.after(V.tensor_tensor(oh, key.rearrange("p (o t) -> p o t", o=1).to_broadcast([P, w, n]),
                                         iota[:, 0:w].rearrange("p (b o) -> p b o", o=1).to_broadcast([P, w, n]), ALU.is_equal))
                st.after(V.tensor_tensor_scan(flat(cu), ones[:, 0:1].to_broadcast([P, w * n]), flat(oh), 0.0,
                                              ALU.mult, ALU.add))
                st.after(V.tensor_copy(cend[:, 1:w + 1], cu[:, :, n - 1]))
                V.tensor_tensor(cnt[:, 0:w], cend[:, 1:w + 1], cend[:, 0:w], ALU.subtract).then_inc(cnt_ready, 1)
                dve.wait_ge(cnt_sum, c + 1)
                st.after(V.tensor_scalar(nt_i[:, 0:w], total_p[:, 0:w], float(P - 1), None, ALU.add))
                st.after(V.tensor_scalar(nt_i[:, 0:w], nt_i[:, 0:w], 7, None, ALU.logical_shift_right))
                st.after(V.tensor_copy(nt[:, 0:w], nt_i[:, 0:w]))
                st.after(V.tensor_tensor_scan(tend[:, 0:w], ones[:, 0:1].to_broadcast([P, w]), nt[:, 0:w], 0.0, ALU.mult, ALU.add))
                st.after(V.tensor_tensor(base[:, 0:w], tend[:, 0:w], nt[:, 0:w], ALU.subtract))
                st.after(V.scalar_tensor_tensor(base[:, 0:w], base[:, 0:w], float(P), before_p[:, 0:w], ALU.mult, ALU.add))
                st.after(V.scalar_tensor_tensor(base[:, 0:w], base[:, 0:w], -1.0, cend[:, 0:w], ALU.add, ALU.subtract))
                st.after(V.tensor_scalar(le[:, 0:w], tend[:, 0:w], part[:, 0:1], None, ALU.is_le))
                st.after(V.tensor_tensor(le[:, 0:w], le[:, 0:w], weight, ALU.mult))
                V.reduce_sum(off[:, :], le[:, 0:w], axis=AXX).then_inc(off_ready, 1)
                st.after(V.tensor_tensor(cu, cu, base[:, 0:w].rearrange("p (b o) -> p b o", o=1).to_broadcast([P, w, n]), ALU.add))
                st.after(V.tensor_tensor(cu, cu, oh, ALU.mult))
                st.after(V.reduce_sum(pos[:, 0:n], cu.rearrange("p b t -> p t b"), axis=AXX))
                row_of()
                dve.wait_ge(off_row, c + 1)
                V.tensor_scalar(table_out, table_p, last, None, ALU.min).then_inc(table_ready, 1)

            def rank_edges(c):
                def rows():
                    st.after(V.tensor_copy(pos_i[:, :], pos[:, :]))
                    st.after(V.tensor_scalar(pos_h[:, :], pos_i[:, :], 7, None, ALU.logical_shift_right))
                    st.after(V.tensor_scalar(pos_l[:, :], pos_i[:, :], P - 1, None, ALU.bitwise_and))
                    st.after(V.tensor_scalar(pos_l[:, :], pos_l[:, :], float(ST), None, ALU.mult))
                    st.after(V.tensor_tensor(pos[:, :], pos_l[:, :], pos_h[:, :], ALU.add))
                    V.tensor_tensor(rows_i[:, ds(c * CT, CT)], pos[:, :], chunk_base[:, ds(c, 1)].to_broadcast([P, CT]),
                                    ALU.add).then_inc(rows_ready, 1)
                rank(blk[:, ds(c * CT, CT)], CT, NB, c, rows, slot_w[:, :], float(4 * BANK),
                     None, table[0:1, ds(c, 1), :].rearrange("a o t -> a (o t)"))

            st.after(V.tensor_scalar(chunk_base[:, :], iota[:, 0:CHUNKS], float(P * ST), None, ALU.mult))
            n0 = st.n
            rank_edges(0)
            steps = st.n - n0

            dve.wait_ge(x_in, 16)
            def block_stats(b, r):
                settled(dve)
                V.bn_stats(stats[:, r, :], xs[:, ds(b, 1), :].rearrange("p o c -> p (o c)")).then_inc(dve_step, 1)

            def group_stats(g):
                st.n = st.n + PRE
                dve.wait_ge(dve_step, st.n)
                settled(dve)
                for r in range(PRE):
                    V.bn_aggr(mv5[:, r, :], stats[:, r, :]).then_inc(dve_step, 1)
                st.n = st.n + PRE
                dve.wait_ge(dve_step, st.n)
                V.tensor_copy(mv[:, ds(PRE * g, PRE), :], mv5[:, :, :]).then_inc(var_ready, 1)
            with dve.Fori(0, NB // PRE) as g:
                def all_stats(g):
                    for r in range(PRE):
                        block_stats(PRE * g + r, r)
                    group_stats(g)
                st.loop(g, 0, NB // PRE, 2 * PRE, all_stats)
            dve.wait_ge(std_ready, 1)
            st.after(V.reciprocal(rstd[:, :], rstd[:, :]))
            def normed(b, r, ready):
                xb = xs[:, ds(b, 1), :].rearrange("p o c -> p (o c)")
                V.tensor_scalar(nrm[:, r, :], xb, mv[:, ds(b, 1), 0], rstd[:, ds(b, 1)], ALU.subtract, ALU.mult
                                ).then_inc(ready, 1)
                return xb
            with dve.Fori(0, NB // PRE) as g:
                def norm(g):
                    dve.wait_ge(tr_done, 1 + PRE * g)
                    for r in range(PRE):
                        xb = normed(PRE * g + r, r, xn_ready)
                        dve.wait_ge(xn_ready, PRE * g + r + 1)
                        st.after(V.tensor_tensor(xb, xb, nrm[:, r, :], ALU.add))
                st.loop(g, 0, NB // PRE, PRE, norm)
            rank_edges(1)

            def node_onehots(s):
                dve.wait_ge(edges_in, 16 * s)
                settled(dve)
                with dve.Fori(0, PAIRS) as i:
                    for r in range(GRPS):
                        m = (s - 1) * PAIRS + i
                        dve.wait_ge(oh_used[r], 1 + m)
                        rowsv = edges_sb[:, ds((i * GRPS + r) * GRP * ROW, GRP * ROW)].rearrange("p (j f) -> p j f", f=ROW)
                        V.tensor_tensor(node_oh[:, r, :].rearrange("p (j n) -> p j n", n=P),
                                        rowsv[:, :, ROW - 1:ROW].to_broadcast([P, GRP, P]),
                                        iota[:, :].rearrange("p (o n) -> p o n", o=1).to_broadcast([P, GRP, P]),
                                        ALU.is_equal).then_inc(oh_ready[r], 1)
            with dve.Fori(1, CHUNKS - 1) as s:
                def mid(s):
                    rank_edges(s + 1)
                    node_onehots(s)
                st.loop(s, 1, CHUNKS - 1, steps, mid)
            node_onehots(CHUNKS - 1)
            node_onehots(CHUNKS)

            for r in range(GRPS):
                dve.wait_ge(oh_used[r], 1 + PAIRS * CHUNKS)
            dve.wait_ge(nf_ready, 1 + NB)
            for k in range(4):
                a, z = k * PER_BANK, min(NB, (k + 1) * PER_BANK)
                sl = slots[:, k, 0:(z - a) * SLOT].rearrange("p (b f) -> p b f", f=SLOT)
                st.after(V.tensor_scalar(rcount[:, a:z], sl[:, :, AD], 1.0, None, ALU.max))
            st.after(V.reciprocal(rcount[:, :], rcount[:, :]))
            for k in range(4):
                a, z = k * PER_BANK, min(NB, (k + 1) * PER_BANK)
                sl = slots[:, k, 0:(z - a) * SLOT].rearrange("p (b f) -> p b f", f=SLOT)
                st.after(V.tensor_tensor(tmean[:, a * AD:z * AD].rearrange("p (b f) -> p b f", f=AD), sl[:, :, 0:AD],
                                         rcount[:, a:z].rearrange("p (b o) -> p b o", o=1).to_broadcast([P, z - a, AD]),
                                         ALU.mult))

            def means(g):
                dve.wait_ge(mt_done, 1 + g)
                V.tensor_copy(mean5[:, :], tmean[:, ds(g * PRE * AD, PRE * AD)]).then_inc(mean_ready, 1)

            def add_group(g):
                for r in range(PRE):
                    b = PRE * g + r
                    xb = xs[:, ds(b, 1), :].rearrange("p o c -> p (o c)")
                    dve.wait_ge(up_done, 1 + b + 1)
                    V.tensor_tensor(xb, xb, up_p[r], ALU.add).then_inc(x1_ready, 1)
                    dve.wait_ge(x1_ready, 1 + b + 1)
                    block_stats(b, r)
                group_stats(g)
            means(0)
            with dve.Fori(0, NB // PRE - 1) as g:
                def step(g):
                    means(g + 1)
                    add_group(g)
                st.loop(g, 0, NB // PRE - 1, 2 * PRE, step)
            add_group(NB // PRE - 1)
            dve.wait_ge(std_ready, 2)
            st.after(V.reciprocal(rstd[:, :], rstd[:, :]))

            def norms(g):
                dve.wait_ge(rt_done, 1 + PRE * g)
                dve.wait_ge(x1n_kept, 1 + PRE * g)
                for r in range(PRE):
                    normed(PRE * g + r, r, x1n_ready)

            def choose(g):
                for r in range(PRE):
                    b = PRE * g + r
                    dve.wait_ge(lg_done, b + 1)
                    lg = lg_p[r]
                    settled(dve)
                    st.after(V.max(top[:, r, :], lg))
                    settled(dve)
                    V.max_index(topi[:, r, :], top[:, r, :], lg).then_inc(lg_used, 1)
                dve.wait_ge(lg_used, 1 + PRE * (g + 1))
                V.tensor_copy(blk[:, ds(PRE * g, PRE)], topi[:, :, 0]).then_inc(chosen, 1)
            norms(0)
            with dve.Fori(0, NB // PRE - 1) as g:
                def both(g):
                    norms(g + 1)
                    choose(g)
                st.loop(g, 0, NB // PRE - 1, PRE, both)
            choose(NB // PRE - 1)
            dve.wait_ge(chosen, NB // PRE)

            def rows():
                V.tensor_copy(rows_i[:, 0:NB], pos[:, 0:NB]).then_inc(tok_rows, 1)
            rank(blk[:, 0:NB], NB, EXPERTS, CHUNKS, rows, ones[:, 0:EXPERTS], float(EXPERTS - 1), None, table[0:1, CHUNKS, :])

            dve.wait_ge(late_in, 16 * 11)
            def results(m, first=False):
                for h in range(2):
                    dve.wait_ge(o_done, 2 * m + h + 1)
                    if not first:
                        dve.wait_ge(stored[h], 16 * m)
                    V.tensor_scalar(tok_res[:, h, :], res_p[h], 0.0, None, ALU.max).then_inc(o_ready, 1)
            results(0, first=True)
            with dve.Fori(1, XT // 2) as m:
                results(m)
            for b in range(NB):
                dve.wait_ge(gathered[b // 5], 16 * 5)
                V.tensor_tensor(xs[:, b, :], xs[:, b, :], x1n[:, b, :], ALU.add).then_inc(y_ready, 1)

        @block.tensor
        def _(pe):
            T = nc.tensor

            def rank_sums(c, w):
                pe.wait_ge(cnt_ready, c + 1)
                T.matmul(before_p[:, 0:w], before[:, :], cnt[:, 0:w], start=True, stop=True)
                T.matmul(total_p[:, 0:w], ones[:, :], cnt[:, 0:w], start=True, stop=True).then_inc(cnt_sum, 1)
                pe.wait_ge(off_ready, c + 1)
                T.matmul(table_p, off[:, 0:1], ident[:, :], start=True, stop=True).then_inc(off_row, 1)

            def time_features(q):
                for h in range(2):
                    pe.wait_ge(attr_in[h], 16 * (q + 1))
                    pe.wait_ge(ring_ready[h], 1 + 3 * q)
                    for j in range(BATCH):
                        last = T.matmul(tfp[:, h * BANK + j * AD:h * BANK + (j + 1) * AD], attr_sb[:, h, j * P:(j + 1) * P],
                                        wt_sb[:, :], start=True, stop=True)
                    last.then_inc(tf_done[h], 1)

            def reduce_groups(c, i):
                for r in range(GRPS):
                    t0 = (i * GRPS + r) * GRP
                    _, offs = nc.values_load_multi_w_load_instructions(
                        table[0:1, ds(c, 1), ds(t0, GRP)].rearrange("a o t -> a (o t)"), engines=[mybir.EngineType.PE],
                        min_val=0, max_val=3 * BANK + 4 * SLOT,
                        skip_runtime_bounds_check_because="a sum of slot widths up to the spare slot")
                    pe.wait_ge(oh_ready[r], c * PAIRS + i + 1)
                    for j in range(GRP):
                        last = T.matmul(sums[:, ds(offs[j], AD + 1)], node_oh[:, r, j * P:(j + 1) * P],
                                        edges_sb[:, ds((t0 + j) * ROW, AD + 1)], start=False, stop=True, skip_group_check=True)
                    last.then_inc(oh_used[r], 1)

            pe.wait_ge(consts, 5)
            pe.wait_ge(ones_set, 1)
            pe.wait_ge(gw_in, 32)
            rank_sums(0, NB)
            pe.wait_ge(mw_in, 32)

            def transpose_norm(r, to, ready, done):
                for k in range(2):
                    last = T.transpose(to[:, k * P:(k + 1) * P], nrm[:, r, k * P:(k + 1) * P], ident[:, :])
                last.then_inc(done, 1)

            def prepare(b, r):
                pe.wait_ge(xn_ready, b + 1)
                pe.wait_ge(tr_copied, 1 + b)
                transpose_norm(r, trp, xn_ready, tr_done)
                pe.wait_ge(tr_copied, 1 + b + 1)
                pe.wait_ge(nf_ready, 1 + b)
                for k in range(2):
                    last = T.matmul(nf_p, wd_sb[:, k, :], xT[:, 0, k * P:(k + 1) * P], start=(k == 0), stop=(k == 1))
                last.then_inc(nf_done, 1)

            with pe.Fori(0, NB // PRE) as i:
                time_features(i)
                for r in range(PRE):
                    prepare(i * PRE + r, r)
            rank_sums(1, NB)
            with pe.Fori(NB // PRE, PAIRS) as i:
                time_features(i)
            pe.wait_ge(nf_ready, 1 + NB)
            for k in range(4):
                T.matmul(slots[:, k, :], zrow[:, 0:P], zrow, start=True, stop=True)

            with pe.Fori(1, CHUNKS - 1) as s:
                rank_sums(s + 1, NB)
                with pe.Fori(0, PAIRS) as i:
                    time_features(s * PAIRS + i)
                    pe.wait_ge(table_ready, s)
                    pe.wait_ge(edges_in, 16 * s)
                    reduce_groups(s - 1, i)
            with pe.Fori(0, PAIRS) as i:
                time_features((CHUNKS - 1) * PAIRS + i)
                pe.wait_ge(table_ready, CHUNKS - 1)
                pe.wait_ge(edges_in, 16 * (CHUNKS - 1))
                reduce_groups(CHUNKS - 2, i)
            pe.wait_ge(table_ready, CHUNKS)
            pe.wait_ge(edges_in, 16 * CHUNKS)
            with pe.Fori(0, PAIRS) as i:
                reduce_groups(CHUNKS - 1, i)

            pe.wait_ge(late_in, 16 * 11)
            with pe.Fori(0, NB // PRE) as g:
                pe.wait_ge(mean_ready, g + 1)
                pe.wait_ge(mt_copied, 1 + 2 * g)
                settled(pe)
                for r in range(PRE):
                    last = T.transpose(tfp[0:AD, r * P:(r + 1) * P], mean5[:, r * AD:(r + 1) * AD], ident[:, :])
                last.then_inc(mt_done, 1)
                pe.wait_ge(mt_copied, 1 + 2 * g + 2)
                pe.wait_ge(fu_ready, 1 + 2 * g)
                for k in range(2):
                    T.matmul(fused_p[k], wf_sb[:, 0, :, :].rearrange("p a n -> p (a n)"), nfT[:, ds(g * (PRE * P) + k * HALF, HALF)], start=True, stop=False)
                    last = T.matmul(fused_p[k], wf_sb[:, 1, :, :].rearrange("p a n -> p (a n)"), meanT[:, k * HALF:(k + 1) * HALF], start=False, stop=True)
                last.then_inc(fu_done, 1)
                pe.wait_ge(fu_ready, 1 + 2 * g + 2)
                for r in range(PRE):
                    if r in (0, 4):
                        pe.wait_ge(x1_ready, 1 + PRE * g + r // 4)
                    T.matmul(up_p[r], fT[:, r * P:(r + 1) * P], wu_sb[:, :], start=True, stop=True).then_inc(up_done, 1)
            with pe.Fori(0, NB // PRE) as g:
                for r in range(PRE):
                    b = PRE * g + r
                    pe.wait_ge(x1n_ready, b + 1)
                    pe.wait_ge(rt_copied, b if r else b + 1)
                    transpose_norm(r, rt_p[r % 2], x1n_ready, rt_done)
                    pe.wait_ge(rt_copied, 1 + b + 1)
                    pe.wait_ge(lg_used, 1 + PRE * g)
                    lg = lg_p[r]
                    for k in range(2):
                        T.matmul(lg, xT[:, r % 2, k * P:(k + 1) * P], rw_sb[:, k, :], start=(k == 0), stop=False)
                    T.matmul(lg, ones[0:1, :], rb_sb[:, :], start=False, stop=True).then_inc(lg_done, 1)
            rank_sums(CHUNKS, EXPERTS)
            pe.wait_ge(table_ready, CHUNKS + 1)
            pe.wait_ge(b1_in, 16)
            with pe.Fori(0, XT // 2) as m:
                for h in range(2):
                    j = 2 * m + h
                    _, (e,) = nc.values_load_multi_w_load_instructions(
                        table[0:1, CHUNKS, ds(j, 1)], engines=[mybir.EngineType.PE], min_val=0, max_val=EXPERTS - 1,
                        skip_runtime_bounds_check_because="clamped to the last expert")
                    pe.wait_ge(tok_loaded[h], 16 * (m + 1))
                    for k in range(2):
                        last = T.transpose(trp[:, k * P:(k + 1) * P], tok_in[:, h, k * P:(k + 1) * P], ident[:, :])
                    last.then_inc(tok_tr, 1)
                    pe.wait_ge(tok_trc, j + 1)
                    for k in range(2):
                        T.matmul(mmp[:, 0:AD], xT[:, 0, k * P:(k + 1) * P], w1_sb[:, ds(e * (2 * AD) + k * AD, AD)],
                                 start=(k == 0), stop=False)
                    T.matmul(mmp[:, 0:AD], ones[0:1, :], b1_sb[:, ds(e * AD, AD)], start=False, stop=True).then_inc(hid_done, 1)
                    pe.wait_ge(hid_ready, j + 1)
                    settled(pe)
                    T.transpose(trp[0:AD, 256:256 + P], hid[:, 0, :], ident[:, :]).then_inc(ht_done, 1)
                    pe.wait_ge(ht_ready, j + 1)
                    pe.wait_ge(o_ready, 1 + j)
                    T.matmul(res_p[h], fT[:, 0:P], w2_sb[:, ds(e * CH, CH)], start=True, stop=True).then_inc(o_done, 1)


_ARGS = ["x", "src", "attr_t", "wd_t", "bd", "wt_t", "bt", "wf_t", "bf", "wu_t", "bu", "rw_t", "rb", "w1", "b1", "w2", "b2"]


def kernel(**inputs):
    import concourse.bacc as bacc
    from concourse.bass_utils import run_bass_kernel_spmd

    a = {k: np.ascontiguousarray(v) for k, v in inputs.items()}
    c = np.ascontiguousarray
    x = np.zeros((NB * P, CH), a["x"].dtype)
    x[:NODES] = a["x"]
    src = np.full((ET * P,), NB * P - 1, a["src"].dtype)
    src[:EDGES] = a["src"]
    attr = np.zeros((ET * P, ED), a["edge_attr_32"].dtype)
    attr[:EDGES] = a["edge_attr_32"]
    arrays = {
        "x": x, "src": src,
        "attr_t": c(attr.reshape(P, ET, ED).transpose(2, 1, 0)).reshape(ED, ET * P),
        "wd_t": c(a["L0_gnn_W_down"].T), "bd": a["L0_gnn_b_down"].reshape(AD, 1),
        "wt_t": c(a["L0_gnn_W_time"].T), "bt": a["L0_gnn_b_time"].reshape(1, AD),
        "wf_t": c(a["L0_gnn_W_fusion"].T), "bf": a["L0_gnn_b_fusion"].reshape(AD, 1),
        "wu_t": c(a["L0_gnn_W_up"].T), "bu": a["L0_gnn_b_up"].reshape(1, CH),
        "rw_t": c(a["L0_ffn_router_w"].T), "rb": a["L0_ffn_router_b"].reshape(1, EXPERTS),
        "w1": a["L0_ffn_W1"], "b1": a["L0_ffn_b1"].reshape(1, EXPERTS * AD),
        "w2": a["L0_ffn_W2"], "b2": a["L0_ffn_b2"].reshape(1, EXPERTS * CH),
    }
    nc = bacc.Bacc("TRN2", target_bir_lowering=False, num_devices=1)
    maps, aps = {}, []
    for name in _ARGS:
        maps[f"{name}_dram"] = arrays[name]
        aps.append(nc.dram_tensor(f"{name}_dram", arrays[name].shape, mybir.dt.from_np(arrays[name].dtype),
                                  kind="ExternalInput").ap())
    out = nc.dram_tensor("out_dram", (NODES, CH), f32, kind="ExternalOutput").ap()
    program(nc, *aps, out)
    r = run_bass_kernel_spmd(nc, [maps], core_ids=[0])
    return r.results[0]["out_dram"]
```

```python
from contextlib import ExitStack

import numpy as np
import concourse.bass as bass
from concourse import mybir

P = 128
NODES, CH, EDGES, ED = 3125, 256, 50000, 32
AD = 64
EXPERTS = 32
NB = -(-NODES // P)
CHUNKS, PAIRS, BATCH = 7, 4, 7
CT = PAIRS * 2 * BATCH
ET = CHUNKS * CT
GRP, GRPS = 4, 5
PIECE = GRPS * GRP
ST = PAIRS * PIECE
assert ET * P >= EDGES and ST >= CT + NB - 1 and ST <= P
ROW = AD + 2
PER_BANK, SLOT = 7, 72
BANK = 512
XT = NB + EXPERTS - 1
PRE = 5
NG = NB // PRE
assert NB % PRE == 0
RING = 4
EPS = 1e-5

f32, bf16, i32, u32 = mybir.dt.float32, mybir.dt.bfloat16, mybir.dt.int32, mybir.dt.uint32
ALU, ACT = mybir.AluOpType, mybir.ActivationFunctionType
AXX = mybir.AxisListType.X
ds = bass.ds


class Count:

    def __init__(self, eng, sem):
        self.eng, self.sem, self.n = eng, sem, 0

    def after(self, ins):
        ins.then_inc(self.sem, 1)
        self.n = self.n + 1
        self.eng.wait_ge(self.sem, self.n)

    def loop(self, i, start, stop, steps, body):
        n0 = self.n
        self.n = n0 + (i - start) * steps
        base = self.n
        body(i)
        self.n = n0 + (stop - start) * steps


def program(nc, x, src, attr_3, attr_1, wd_t, bd, wt_t, bt, wf_t, bf, wu_t, bu, rw_t, rb, w1, b1, w2, b2, out):
    ctx = ExitStack()
    with ctx:
        def sb(name, shape, dt=f32):
            return ctx.enter_context(nc.sbuf_tensor(name, shape, dt))

        def sem(name):
            return ctx.enter_context(nc.semaphore(name))

        edges_sorted = nc.dram_tensor("edges_sorted", (CHUNKS * P * ST, ROW), f32, kind="Internal").ap()
        tok_sorted = nc.dram_tensor("tok_sorted", (XT * P, CH), f32, kind="Internal").ap()
        tok_out = nc.dram_tensor("tok_out", (XT * P, CH), f32, kind="Internal").ap()

        table = sb("table", [1, CHUNKS + 1, P], i32)
        ident = sb("ident", [P, P])
        ones = sb("ones", [P, P])
        before = sb("before", [P, P])
        iota_i = sb("iota_i", [P, P], i32)
        iota = sb("iota", [P, P])
        part_i = sb("part_i", [P, 1], i32)
        part = sb("part", [P, 1])
        slot_w = sb("slot_w", [P, NB])
        empty_row = sb("empty_row", [P, PIECE * ROW])
        zeros = sb("zeros", [P, 2 * CH])
        zrow = zeros[0:1, 0:BANK]
        epsb = sb("epsb", [P, 1])
        chunk_base = sb("chunk_base", [P, CHUNKS])

        src_i = sb("src_i", [P, ET], i32)
        tmp_i = sb("tmp_i", [P, ET], i32)
        blk = sb("blk", [P, ET])
        lo = sb("lo", [P, ET])
        rows_i = sb("rows_i", [P, ET], i32)
        onehot = sb("onehot", [P, NB, CT], bf16)
        cum = sb("cum", [P, NB, CT])
        pos = sb("pos", [P, CT])
        pos_i = sb("pos_i", [P, CT], i32)
        pos_h = sb("pos_h", [P, CT], i32)
        pos_l = sb("pos_l", [P, CT], i32)
        cend = sb("cend", [P, EXPERTS + 1])
        cnt = sb("cnt", [P, EXPERTS])
        nt_i = sb("nt_i", [P, EXPERTS], i32)
        nt = sb("nt", [P, EXPERTS])
        tend = sb("tend", [P, EXPERTS])
        base = sb("base", [P, EXPERTS])
        le = sb("le", [P, EXPERTS])
        off = sb("off", [P, 1])
        

        attr_sb = sb("attr_sb", [3 * ED + 1, 2, 3 * P])
        ring = sb("ring", [P, 2, BATCH * ROW])
        idx_ring = sb("idx_ring", [P, 2, BATCH], u32)
        edges_sb = sb("edges_sb", [P, 2, PIECE * ROW])
        node_oh = sb("node_oh", [P, GRPS, GRP * P])

        bt_sb = sb("bt_sb", [1, AD])
        wd_sb = sb("wd_sb", [P, 2, AD])
        bd_sb = sb("bd_sb", [AD, 1])
        wt_sb = sb("wt_sb", [3 * ED + 1, 3 * AD])
        wf_sb = sb("wf_sb", [P, AD])
        bf_sb = sb("bf_sb", [AD, 1])
        wu_sb = sb("wu_sb", [AD + 1, CH])
        rw_sb = sb("rw_sb", [P, 2, EXPERTS])
        rb_sb = sb("rb_sb", [1, EXPERTS])
        b1_sb = sb("b1_sb", [1, EXPERTS * AD])
        w1_sb = sb("w1_sb", [P, EXPERTS * 2 * AD])
        w2_sb = sb("w2_sb", [AD + 1, EXPERTS * CH])

        xs = sb("xs", [P, NB, CH])
        x1n = sb("x1n", [P, NB, CH])
        nrm = sb("nrm", [P, PRE, CH])
        flat_n = x1n[:, :, :].rearrange("p b c -> p (b c)")
        tmean = flat_n[:, 0:NB * AD]
        combT = flat_n[:, NB * AD:NB * (AD + P)]
        mean5 = sb("mean5", [P, PRE, 2 * AD])
        stats = sb("stats", [P, PRE, 6])
        mv5 = sb("mv5", [P, PRE, 2])
        mv = sb("mv", [P, NB, 2])
        rstd = sb("rstd", [P, NB])
        rcount = sb("rcount", [P, NB])
        xT = sb("xT", [P, 3, 2 * P])
        fT = sb("fT", [AD + 1, PRE * P])
        top = sb("top", [P, PRE, 8])
        topi = sb("topi", [P, PRE, 8], u32)
        hid = sb("hid", [P, 2, AD])
        tok_in = sb("tok_in", [P, RING, CH])
        tok_res = sb("tok_res", [P, RING, CH])

        sums = ctx.enter_context(nc.psum_tensor("sums", [P, 4 * BANK], f32))
        tfp = ctx.enter_context(nc.psum_tensor("tfp", [P, 2 * BANK], f32))
        trp = ctx.enter_context(nc.psum_tensor("trp", [P, BANK], f32))
        mmp = ctx.enter_context(nc.psum_tensor("mmp", [P, BANK], f32))
        banks = [sums[:, k * BANK:(k + 1) * BANK] for k in range(4)]
        tf_p = [tfp[:, h * BANK:(h + 1) * BANK] for h in range(2)]
        HALF = PRE * P // 2
        fused_p = [mmp[0:AD, 0:HALF], trp[0:AD, 0:HALF]]
        up_p = [banks[r % 4][:, 0:CH] for r in range(PRE)]
        lg_p = [b[:, 0:EXPERTS] for b in (*banks, trp[:, :])]
        rt_p = [b[:, 0:2 * P] for b in (*tf_p, mmp)]
        nf_p = banks[0][0:AD, 0:P]
        tok_p = [b[:, 0:2 * P] for b in tf_p]
        hid_p = [b[:, 0:AD] for b in (mmp, trp)]
        hT_p = [b[0:AD, 0:P] for b in banks[2:4]]
        res_p = [b[:, 0:CH] for b in banks[0:2]]
        slots = sums[:, :].rearrange("p (k c) -> p k c", k=4)
        before_p, total_p, table_p = mmp[:, 0:EXPERTS], mmp[:, 64:64 + EXPERTS], mmp[0:1, 128:256]

        consts = sem("consts")
        ones_set = sem("ones_set")
        src_in, x_in, gw_in, mw_in, late_in = sem("src_in"), sem("x_in"), sem("gw_in"), sem("mw_in"), sem("late_in")
        cleared = sem("cleared")
        tok_cleared = sem("tok_cleared")
        wt_zero = sem("wt_zero")
        attr_in = [sem(f"attr_in{h}") for h in range(2)]
        tf_done = [sem(f"tf_done{h}") for h in range(2)]
        ring_ready = [sem(f"ring_ready{h}") for h in range(2)]
        scattered = [sem(f"scattered{h}") for h in range(2)]
        edges_in = [sem(f"edges_in{h}") for h in range(2)]
        oh_ready = [sem(f"oh_ready{r}") for r in range(GRPS)]
        oh_used = [sem(f"oh_used{r}") for r in range(GRPS)]
        dve_step, act_step, pe_step, pool_step = sem("dve_step"), sem("act_step"), sem("pe_step"), sem("pool_step")
        cnt_ready, cnt_sum, off_ready, off_row, table_ready, rows_ready = (
            sem("cnt_ready"), sem("cnt_sum"), sem("off_ready"), sem("off_row"), sem("table_ready"), sem("rows_ready"))
        var_ready, std_ready, xn_ready = sem("var_ready"), sem("std_ready"), sem("xn_ready")
        tr_done, tr_copied, nf_done, nf_ready = sem("tr_done"), sem("tr_copied"), sem("nf_done"), sem("nf_ready")
        mean_ready, mt_done, mt_copied, fu_done, fu_ready, up_done, x1_ready = (
            sem("mean_ready"), sem("mt_done"), sem("mt_copied"), sem("fu_done"), sem("fu_ready"), sem("up_done"), sem("x1_ready"))
        chosen, x1n_kept = sem("chosen"), sem("x1n_kept")
        x1n_ready, rt_done, rt_copied, lg_done, lg_used = (
            sem("x1n_ready"), sem("rt_done"), sem("rt_copied"), sem("lg_done"), sem("lg_used"))
        tok_rows, tok_scat = sem("tok_rows"), sem("tok_scat")
        tok_loaded = [sem(f"tok_loaded{h}") for h in range(RING)]
        tok_tr, tok_trc, hid_done, hid_ready, ht_done, ht_ready, o_done, o_ready = (
            sem("tok_tr"), sem("tok_trc"), sem("hid_done"), sem("hid_ready"), sem("ht_done"), sem("ht_ready"),
            sem("o_done"), sem("o_ready"))
        stored = [sem(f"stored{h}") for h in range(RING)]
        gathered = [sem(f"gathered{h}") for h in range(5)]
        y_ready = sem("y_ready")
        y_out = sem("y_out")

        started = {f: 1 for f in (*ring_ready, tr_copied, nf_ready, tr_done, fu_ready, x1_ready, up_done,
                                  mt_done, rt_copied, lg_used, rt_done)}
        started |= {f: 2 for f in (*oh_used, lg_done)}

        def settled(eng):
            eng.sem_inc(passed[eng.engine], 1)

        passed = {eng.engine: sem(f"passed_{name}") for name, eng in
                  (("dve", nc.vector), ("pool", nc.gpsimd), ("pe", nc.tensor))}

        def expert_steps(eng, step, group=None):
            def steps(t, n=RING):
                values = (group(t),) if group else ()
                for r in range(n):
                    step(t + r, r, *values)
            steps(0)
            steps(RING)
            with eng.Fori(2, XT // RING) as m:
                steps(m * RING)
            steps(XT, 3)

        LATE = 7 + 4 * 3
        block = ctx.enter_context(nc.Block())

        @block.sync
        def _(sp):
            sp.dma_start(src_i[:, :], src.rearrange("(p t) -> p t", p=P)).then_inc(src_in, 16)
            def clear(c, i):
                dst = edges_sorted[:, :].rearrange("(c p j) f -> c p (j f)", c=CHUNKS, p=P)
                sp.dma_start(dst[ds(c, 1), :, i * PIECE * ROW:(i + 1) * PIECE * ROW].rearrange("o p n -> (o p) n"),
                             empty_row[:, :]).then_inc(cleared, 16)

            def attributes(q, first=False):
                for h in range(2):
                    if not first:
                        sp.wait_ge(tf_done[h], q)
                    sp.dma_start(attr_sb[0:3 * ED, h, 0:2 * P], attr_3[:, ds((2 * q + h) * 2 * P, 2 * P)]).then_inc(attr_in[h], 16)
                    sp.dma_start(attr_sb[0:ED, h, 2 * P:3 * P], attr_1[:, ds((2 * q + h) * P, P)]).then_inc(attr_in[h], 16)

            def load_piece(c, i):
                if i == 0:
                    for h in range(2):
                        sp.wait_ge(scattered[h], BATCH * 16 * PAIRS * (c + 1))
                sp.wait_ge(oh_used[-1], 1 + PAIRS * c + i)
                sp.dma_start(edges_sb[:, i % 2, :], edges_sorted[:, :].rearrange("(c p j) f -> c p (j f)", c=CHUNKS, p=P)
                             [ds(c, 1), :, i * PIECE * ROW:(i + 1) * PIECE * ROW].rearrange("o p n -> (o p) n")
                             ).then_inc(edges_in[i % 2], 16)

            attributes(0, first=True)
            sp.wait_ge(wt_zero, 1)
            sp.wait_ge(consts, 1)
            for i in range(PAIRS):
                clear(0, i)
            for k in range(3):
                sp.dma_start(wt_sb[k * ED:(k + 1) * ED, k * AD:(k + 1) * AD], wt_t).then_inc(gw_in, 16)
                sp.dma_start(wt_sb[3 * ED:3 * ED + 1, k * AD:(k + 1) * AD], bt).then_inc(gw_in, 16)
            sp.dma_start(bt_sb[:, :], bt).then_inc(gw_in, 16)
            sp.dma_start(xs[:, :, :], x.rearrange("(b p) c -> p b c", p=P)).then_inc(x_in, 16)
            sp.dma_start(wd_sb[:, :, :], wd_t.rearrange("(k p) n -> p k n", p=P)).then_inc(mw_in, 16)
            sp.dma_start(bd_sb[:, :], bd).then_inc(mw_in, 16)
            sp.wait_ge(cleared, 16 * PAIRS)
            clear(1, 0)
            for i in range(1, PAIRS):
                attributes(i)
                clear(1, i)
            sp.dma_start(wf_sb[:, :], wf_t).then_inc(late_in, 16)
            sp.dma_start(bf_sb[:, :], bf).then_inc(late_in, 16)
            sp.dma_start(wu_sb[0:AD, :], wu_t).then_inc(late_in, 16)
            sp.dma_start(wu_sb[AD:AD + 1, :], bu).then_inc(late_in, 16)
            sp.dma_start(rw_sb[:, :, :], rw_t.rearrange("(k p) n -> p k n", p=P)).then_inc(late_in, 16)
            sp.dma_start(rb_sb[:, :], rb).then_inc(late_in, 16)
            sp.dma_start(b1_sb[:, :], b1).then_inc(late_in, 16)

            def stage(s, ahead=None):
                for i in range(PAIRS):
                    attributes(PAIRS * s + i)
                    if ahead:
                        ahead(s, i)
                    if i == 0:
                        load_piece(s - 1, 0)
                        load_piece(s - 1, 1)
                    elif i < PAIRS - 1:
                        load_piece(s - 1, i + 1)

            def clear_next(s, i):
                if i == 0:
                    sp.wait_ge(cleared, 16 * PAIRS * (s + 1))
                clear(s + 1, i)

            def share(s, i):
                clear_next(s, i)
                if i == 0:
                    n = EXPERTS // 4 * 2 * AD
                    sp.dma_start(w1_sb[:, ds((s - 1) * n, n)], w1[:, ds((s - 1) * n, n)]).then_inc(late_in, 16)
                elif i == 1:
                    n = EXPERTS // 4 * CH
                    sp.dma_start(w2_sb[0:AD, ds((s - 1) * n, n)], w2[:, ds((s - 1) * n, n)]).then_inc(late_in, 16)
                    sp.dma_start(w2_sb[AD:AD + 1, ds((s - 1) * n, n)], b2[:, ds((s - 1) * n, n)]).then_inc(late_in, 16)
                elif i == 2:
                    dst = tok_sorted[:, :].rearrange("(s p k j) c -> s p k (j c)", s=4, p=P, j=2)
                    sp.dma_start(dst[ds(s - 1, 1)].rearrange("o p k n -> (o p) k n"),
                                 zeros[:, :].rearrange("p (o n) -> p o n", o=1).to_broadcast([P, XT // 8, 2 * CH])
                                 ).then_inc(tok_cleared, 16)

            with sp.Fori(1, 5) as s:
                stage(s, share)
            stage(5, clear_next)
            stage(6)
            for i in range(PAIRS):
                load_piece(CHUNKS - 1, i)

            sp.wait_ge(tok_scat, 16 * NB)
            def load_tile(t, r, first=False):
                if not first:
                    sp.wait_ge(tok_tr, t - RING + 1)
                sp.dma_start(tok_in[:, r, :], tok_sorted[ds(t * P, P), :]).then_inc(tok_loaded[r], 16)
            for r in range(RING):
                load_tile(r, r, first=True)
            with sp.Fori(1, XT // RING) as m:
                for r in range(RING):
                    load_tile(m * RING + r, r)

            with sp.Fori(0, NODES // P) as b:
                sp.wait_ge(y_ready, b + 1)
                sp.dma_start(out[ds(b * P, P), :], xs[:, ds(b, 1), :].rearrange("p o c -> p (o c)")).then_inc(y_out, 16)
            sp.wait_ge(y_ready, NB)
            sp.dma_start(out[NODES // P * P:NODES, :], xs[0:NODES % P, NB - 1, :]).then_inc(y_out, 16)
            sp.wait_ge(y_out, 16 * NB)

        @block.gpsimd
        def _(pool):
            for freed, n in started.items():
                pool.sem_inc(freed, n)
            pool.memset(empty_row[:, :].rearrange("p (j f) -> p j f", f=ROW)[:, :, 0:ROW - 1], 0.0).then_inc(pool_step, 1)
            pool.memset(zeros[:, :], 0.0).then_inc(pool_step, 1)
            pool.wait_ge(pool_step, 2)
            pool.memset(empty_row[:, :].rearrange("p (j f) -> p j f", f=ROW)[:, :, ROW - 1:ROW], -1.0).then_inc(consts, 1)
            pool.iota(iota_i[:, :], pattern=[[1, P]], base=0, channel_multiplier=0).then_inc(consts, 1)
            pool.iota(part_i[:, :], pattern=[[1, 1]], base=0, channel_multiplier=1).then_inc(consts, 1)
            pool.memset(ident[:, :], 0.0).then_inc(pool_step, 1)
            pool.memset(before[:, :], 0.0).then_inc(pool_step, 1)
            pool.wait_ge(pool_step, 4)
            pool.affine_select(out=before[:, :], in_=before[:, :], compare_op=ALU.is_ge, fill=1.0,
                               base=0, pattern=[[-1, P]], channel_multiplier=1).then_inc(consts, 1)
            pool.affine_select(out=ident[:, :], in_=ident[:, :], compare_op=ALU.not_equal, fill=1.0,
                               base=0, pattern=[[-1, P]], channel_multiplier=1).then_inc(consts, 1)

            with pool.Fori(0, CHUNKS) as s:
                pool.wait_ge(cleared, 16 * PAIRS * (s + 1))
                settled(pool)
                with pool.Fori(0, PAIRS) as i:
                    for h in range(2):
                        pool.wait_ge(ring_ready[h], 1 + 3 * (PAIRS * s + i + 1))
                        settled(pool)
                        for j in range(BATCH):
                            pool.indirect_dma_start(
                                edges_sorted[:, :], bass.IndirectOffsetOnAxis(ap=idx_ring[:, h, j:j + 1], axis=0),
                                ring[:, h, j * ROW:(j + 1) * ROW], None).then_inc(scattered[h], 16)

            pool.wait_ge(x1n_kept, NB)
            pool.wait_ge(tok_cleared, 64)
            pool.wait_ge(tok_rows, 1)
            for b in range(NB):
                pool.indirect_dma_start(tok_sorted[:, :], bass.IndirectOffsetOnAxis(ap=rows_i[:, b:b + 1].bitcast(u32), axis=0),
                                        x1n[:, b, :], None).then_inc(tok_scat, 16)
            with pool.Fori(0, XT // RING) as m:
                for r in range(RING):
                    pool.wait_ge(o_ready, m * RING + r + 1)
                    settled(pool)
                    pool.dma_start(tok_out[ds((m * RING + r) * P, P), :], tok_res[:, r, :]).then_inc(stored[r], 16)
            for r in range(RING):
                pool.wait_ge(stored[r], 16 * (XT // RING))
            pool.wait_ge(tok_scat, 16 * NB)
            for b in range(NB):
                pool.indirect_dma_start(x1n[:, b, :], None, tok_out[:, :],
                                        bass.IndirectOffsetOnAxis(ap=rows_i[:, b:b + 1].bitcast(u32), axis=0)
                                        ).then_inc(gathered[b // 5], 16)

        @block.scalar
        def _(act):
            def batches(q, first=False):
                for h in range(2):
                    act.wait_ge(tf_done[h], q + 1)
                    if not first:
                        act.wait_ge(scattered[h], BATCH * 16 * q)
                    r = ring[:, h, :].rearrange("p (j f) -> p j f", f=ROW)
                    act.activation(r[:, :, 0:AD], tfp[:, h * BANK:h * BANK + BATCH * AD].rearrange("p (j f) -> p j f", f=AD),
                                   ACT.Relu).then_inc(ring_ready[h], 1)
                    act.activation(r[:, :, ROW - 1], lo[:, ds((2 * q + h) * BATCH, BATCH)], ACT.Copy).then_inc(ring_ready[h], 1)
                    act.activation(idx_ring[:, h, :], rows_i[:, ds((2 * q + h) * BATCH, BATCH)], ACT.Copy
                                   ).then_inc(ring_ready[h], 1)

            def stdev(n):
                act.wait_ge(var_ready, NB // PRE * n)
                act.activation(rstd[:, :], mv[:, :, 1], ACT.Sqrt, bias=epsb[:, 0:1]).then_inc(std_ready, 1)

            def prepare(b):
                act.wait_ge(tr_done, 1 + b + 1)
                act.activation(xT[:, 0, :], trp[:, 0:2 * P], ACT.Copy).then_inc(tr_copied, 1)
                act.wait_ge(nf_done, b + 1)
                act.activation(combT[0:AD, ds(b * P, P)], nf_p, ACT.Relu, bias=bd_sb[:, 0:1]).then_inc(nf_ready, 1)

            act.wait_ge(ones_set, 1)
            act.wait_ge(rows_ready, 1)
            batches(0, first=True)
            stdev(1)
            act.wait_ge(mw_in, 32)
            for r in range(PRE):
                prepare(r)
            with act.Fori(1, PAIRS) as i:
                batches(i)
                for r in range(PRE):
                    prepare(i * PRE + r)
            for b in range(PAIRS * PRE, NB):
                prepare(b)
            with act.Fori(1, CHUNKS) as s:
                act.wait_ge(rows_ready, s + 1)
                with act.Fori(0, PAIRS) as i:
                    batches(PAIRS * s + i)

            act.wait_ge(late_in, 16 * LATE)

            def means_transposed(g):
                act.wait_ge(mt_done, 1 + g + 1)
                act.activation(combT[AD:P, ds(g * PRE * P, 4 * P)], tf_p[0][AD:P, :], ACT.Copy).then_inc(mt_copied, 1)
                act.activation(combT[AD:P, ds((g * PRE + 4) * P, P)], tf_p[1][AD:P, 0:P], ACT.Copy).then_inc(mt_copied, 1)

            def fused(g):
                act.wait_ge(fu_done, g + 1)
                act.wait_ge(up_done, 1 + PRE * g)
                for k, half in enumerate(fused_p):
                    act.activation(fT[0:AD, k * HALF:(k + 1) * HALF], half, ACT.Relu, bias=bf_sb[:, 0:1]).then_inc(fu_ready, 1)
            means_transposed(0)
            with act.Fori(0, NG - 1) as g:
                fused(g)
                means_transposed(g + 1)
            fused(NG - 1)
            stdev(2)
            with act.Fori(0, NG) as g:
                for r in range(PRE):
                    b = PRE * g + r
                    act.wait_ge(rt_done, 1 + b + 1)
                    act.wait_ge(lg_done, 1 + b)
                    act.activation(xT[:, r % 3, :], rt_p[r % 3], ACT.Copy).then_inc(rt_copied, 1)

            def step(t, r):
                h = r % 2
                if not (isinstance(t, int) and t >= XT):
                    act.wait_ge(tok_tr, t + 1)
                    if not (isinstance(t, int) and t < 2):
                        act.wait_ge(hid_done, t - 1)
                    act.activation(xT[:, h, :], tok_p[h], ACT.Copy).then_inc(tok_trc, 1)
                j = t - 2
                if not (isinstance(t, int) and (j < 0 or j >= XT)):
                    act.wait_ge(ht_done, j + 1)
                    if not (isinstance(t, int) and j < 2):
                        act.wait_ge(o_done, j - 1)
                    act.activation(fT[0:AD, h * P:(h + 1) * P], hT_p[h], ACT.Copy).then_inc(ht_ready, 1)
            expert_steps(act, step)

        @block.vector
        def _(dve):
            st = Count(dve, dve_step)
            V = nc.vector
            dve.wait_ge(consts, 3)
            V.memset(wt_sb[:, :], 0.0).then_inc(wt_zero, 1)
            V.memset(ones[:, :], 1.0).then_inc(dve_step, 1)
            V.memset(attr_sb[3 * ED:3 * ED + 1, :, :], 1.0).then_inc(dve_step, 1)
            V.memset(ring[:, :, :].rearrange("p h (j f) -> p h j f", f=ROW)[:, :, :, AD], 1.0).then_inc(dve_step, 1)
            V.memset(fT[AD:AD + 1, :], 1.0).then_inc(dve_step, 1)
            V.memset(epsb[:, :], EPS).then_inc(dve_step, 1)
            V.memset(cend[:, 0:1], 0.0).then_inc(dve_step, 1)
            V.memset(slot_w[:, :], float(SLOT)).then_inc(dve_step, 1)
            V.tensor_copy(iota[:, :], iota_i[:, :]).then_inc(dve_step, 1)
            V.tensor_copy(part[:, :], part_i[:, :]).then_inc(dve_step, 1)
            st.n = 9
            dve.wait_ge(dve_step, st.n)
            V.memset(slot_w[:, PER_BANK - 1:NB:PER_BANK], float(BANK - (PER_BANK - 1) * SLOT)).then_inc(ones_set, 1)
            dve.wait_ge(ones_set, 1)
            V.memset(mean5[:, :, :], 0.0).then_inc(ones_set, 1)
            dve.wait_ge(src_in, 16)
            st.after(V.tensor_scalar(tmp_i[:, :], src_i[:, :], 7, None, ALU.logical_shift_right))
            st.after(V.tensor_copy(blk[:, :], tmp_i[:, :]))
            st.after(V.tensor_scalar(tmp_i[:, :], src_i[:, :], P - 1, None, ALU.bitwise_and))
            st.after(V.tensor_copy(lo[:, :], tmp_i[:, :]))

            flat = lambda a: a.rearrange("p b t -> p (b t)")

            def ranking(key, n, w, c, row_of, weight, last, table_out):
                oh = flat(onehot[:, :, :])[:, 0:w * n].rearrange("p (b t) -> p b t", t=n)
                cu = flat(cum[:, :, :])[:, 0:w * n].rearrange("p (b t) -> p b t", t=n)

                def count():
                    st.after(V.tensor_tensor(oh, key.rearrange("p (o t) -> p o t", o=1).to_broadcast([P, w, n]),
                                             iota[:, 0:w].rearrange("p (b o) -> p b o", o=1).to_broadcast([P, w, n]),
                                             ALU.is_equal))
                    st.after(V.tensor_tensor_scan(flat(cu), ones[:, 0:1].to_broadcast([P, w * n]), flat(oh), 0.0,
                                                  ALU.mult, ALU.add))
                    st.after(V.tensor_copy(cend[:, 1:w + 1], cu[:, :, n - 1]))
                    V.tensor_tensor(cnt[:, 0:w], cend[:, 1:w + 1], cend[:, 0:w], ALU.subtract).then_inc(cnt_ready, 1)

                def place():
                    dve.wait_ge(cnt_sum, c + 1)
                    st.after(V.tensor_scalar(nt_i[:, 0:w], total_p[:, 0:w], float(P - 1), None, ALU.add))
                    st.after(V.tensor_scalar(nt_i[:, 0:w], nt_i[:, 0:w], 7, None, ALU.logical_shift_right))
                    st.after(V.tensor_copy(nt[:, 0:w], nt_i[:, 0:w]))
                    st.after(V.tensor_tensor_scan(tend[:, 0:w], ones[:, 0:1].to_broadcast([P, w]), nt[:, 0:w], 0.0,
                                                  ALU.mult, ALU.add))
                    st.after(V.tensor_tensor(base[:, 0:w], tend[:, 0:w], nt[:, 0:w], ALU.subtract))
                    st.after(V.scalar_tensor_tensor(base[:, 0:w], base[:, 0:w], float(P), before_p[:, 0:w], ALU.mult, ALU.add))
                    st.after(V.scalar_tensor_tensor(base[:, 0:w], base[:, 0:w], -1.0, cend[:, 0:w], ALU.add, ALU.subtract))
                    st.after(V.tensor_scalar(le[:, 0:w], tend[:, 0:w], part[:, 0:1], None, ALU.is_le))
                    st.after(V.tensor_tensor(le[:, 0:w], le[:, 0:w], weight, ALU.mult))
                    V.reduce_sum(off[:, :], le[:, 0:w], axis=AXX).then_inc(off_ready, 1)
                    st.after(V.tensor_tensor(cu, cu, base[:, 0:w].rearrange("p (b o) -> p b o", o=1).to_broadcast([P, w, n]),
                                             ALU.add))
                    st.after(V.tensor_tensor(cu, cu, oh, ALU.mult))
                    st.after(V.reduce_sum(pos[:, 0:n], cu.rearrange("p b t -> p t b"), axis=AXX))
                    row_of()

                def tabulate():
                    dve.wait_ge(off_row, c + 1)
                    V.tensor_scalar(table_out, table_p, last, None, ALU.min).then_inc(table_ready, 1)
                return count, place, tabulate

            def rank_edges(c):
                def rows():
                    st.after(V.tensor_copy(pos_i[:, :], pos[:, 0:CT]))
                    st.after(V.tensor_scalar(pos_h[:, :], pos_i[:, :], 7, None, ALU.logical_shift_right))
                    st.after(V.tensor_scalar(pos_l[:, :], pos_i[:, :], P - 1, None, ALU.bitwise_and))
                    st.after(V.tensor_scalar(pos_l[:, :], pos_l[:, :], float(ST), None, ALU.mult))
                    st.after(V.tensor_tensor(pos[:, 0:CT], pos_l[:, :], pos_h[:, :], ALU.add))
                    V.tensor_tensor(rows_i[:, ds(c * CT, CT)], pos[:, 0:CT], chunk_base[:, ds(c, 1)].to_broadcast([P, CT]),
                                    ALU.add).then_inc(rows_ready, 1)
                return ranking(blk[:, ds(c * CT, CT)], CT, NB, c, rows, slot_w[:, :], float(4 * BANK),
                               table[0:1, ds(c, 1), :].rearrange("a o t -> a (o t)"))

            st.after(V.tensor_scalar(chunk_base[:, :], iota[:, 0:CHUNKS], float(P * ST), None, ALU.mult))
            n0 = st.n
            for part_of_it in rank_edges(0):
                part_of_it()
            steps = st.n - n0
            for part_of_it in rank_edges(1):
                part_of_it()

            dve.wait_ge(x_in, 16)
            def block_stats(b, r):
                settled(dve)
                V.bn_stats(stats[:, r, :], xs[:, ds(b, 1), :].rearrange("p o c -> p (o c)")).then_inc(dve_step, 1)

            def group_stats(g):
                st.n = st.n + PRE
                dve.wait_ge(dve_step, st.n)
                settled(dve)
                for r in range(PRE):
                    V.bn_aggr(mv5[:, r, :], stats[:, r, :]).then_inc(dve_step, 1)
                st.n = st.n + PRE
                dve.wait_ge(dve_step, st.n)
                V.tensor_copy(mv[:, ds(PRE * g, PRE), :], mv5[:, :, :]).then_inc(var_ready, 1)
            with dve.Fori(0, NG) as g:
                def all_stats(g):
                    for r in range(PRE):
                        block_stats(PRE * g + r, r)
                    group_stats(g)
                st.loop(g, 0, NG, 2 * PRE, all_stats)
            dve.wait_ge(std_ready, 1)
            st.after(V.reciprocal(rstd[:, :], rstd[:, :]))

            def normed(to, b, ready):
                xb = xs[:, ds(b, 1), :].rearrange("p o c -> p (o c)")
                V.tensor_scalar(to, xb, mv[:, ds(b, 1), 0], rstd[:, ds(b, 1)], ALU.subtract, ALU.mult).then_inc(ready, 1)
                return xb
            with dve.Fori(0, NG) as g:
                def norm(g):
                    dve.wait_ge(tr_done, 1 + PRE * g)
                    for r in range(PRE):
                        normed(nrm[:, r, :], PRE * g + r, xn_ready)
                    dve.wait_ge(xn_ready, PRE * g + PRE)
                    group = xs[:, ds(PRE * g, PRE), :]
                    st.after(V.tensor_tensor(group, group, nrm[:, :, :], ALU.add))
                st.loop(g, 0, NG, 1, norm)

            def node_onehots(c, i):
                n = PAIRS * c + i
                dve.wait_ge(edges_in[i % 2], 16 * (PAIRS // 2 * c + i // 2 + 1))
                for r in range(GRPS):
                    dve.wait_ge(oh_used[r], 2 + n)
                    rows = edges_sb[:, i % 2, r * GRP * ROW:(r + 1) * GRP * ROW].rearrange("p (j f) -> p j f", f=ROW)
                    V.tensor_tensor(node_oh[:, r, :].rearrange("p (j n) -> p j n", n=P),
                                    rows[:, :, ROW - 1:ROW].to_broadcast([P, GRP, P]),
                                    iota[:, :].rearrange("p (o n) -> p o n", o=1).to_broadcast([P, GRP, P]),
                                    ALU.is_equal).then_inc(oh_ready[r], 1)
            with dve.Fori(1, CHUNKS - 1) as s:
                def mid(s):
                    parts = rank_edges(s + 1)
                    for i in range(PAIRS):
                        node_onehots(s - 1, i)
                        if i < len(parts):
                            parts[i]()
                st.loop(s, 1, CHUNKS - 1, steps, mid)
            for c in (CHUNKS - 2, CHUNKS - 1):
                for i in range(PAIRS):
                    node_onehots(c, i)

            for r in range(GRPS):
                dve.wait_ge(oh_used[r], 2 + PAIRS * CHUNKS)
            dve.wait_ge(nf_ready, 1 + NB)
            for k in range(4):
                a, z = k * PER_BANK, min(NB, (k + 1) * PER_BANK)
                sl = slots[:, k, 0:(z - a) * SLOT].rearrange("p (b f) -> p b f", f=SLOT)
                st.after(V.tensor_scalar(rcount[:, a:z], sl[:, :, AD], 1.0, None, ALU.max))
            st.after(V.reciprocal(rcount[:, :], rcount[:, :]))
            for k in range(4):
                a, z = k * PER_BANK, min(NB, (k + 1) * PER_BANK)
                sl = slots[:, k, 0:(z - a) * SLOT].rearrange("p (b f) -> p b f", f=SLOT)
                st.after(V.tensor_tensor(tmean[:, a * AD:z * AD].rearrange("p (b f) -> p b f", f=AD), sl[:, :, 0:AD],
                                         rcount[:, a:z].rearrange("p (b o) -> p b o", o=1).to_broadcast([P, z - a, AD]),
                                         ALU.mult))

            def means(g):
                dve.wait_ge(mt_done, 1 + g)
                V.tensor_copy(mean5[:, :, AD:2 * AD], tmean[:, ds(g * PRE * AD, PRE * AD)].rearrange("p (b f) -> p b f", f=AD)
                              ).then_inc(mean_ready, 1)

            def add_group(g):
                for r in range(PRE):
                    b = PRE * g + r
                    xb = xs[:, ds(b, 1), :].rearrange("p o c -> p (o c)")
                    dve.wait_ge(up_done, 1 + b + 1)
                    V.tensor_tensor(xb, xb, up_p[r], ALU.add).then_inc(x1_ready, 1)
                    dve.wait_ge(x1_ready, 1 + b + 1)
                    block_stats(b, r)
                group_stats(g)
            means(0)
            with dve.Fori(0, NB // PRE - 1) as g:
                def step(g):
                    means(g + 1)
                    add_group(g)
                st.loop(g, 0, NB // PRE - 1, 2 * PRE, step)
            add_group(NB // PRE - 1)
            dve.wait_ge(std_ready, 2)
            st.after(V.reciprocal(rstd[:, :], rstd[:, :]))

            def norms(g):
                dve.wait_ge(rt_done, 1 + PRE * g)
                for r in range(PRE):
                    normed(nrm[:, r, :], PRE * g + r, x1n_ready)
                for r in range(PRE):
                    normed(x1n[:, ds(PRE * g + r, 1), :].rearrange("p o c -> p (o c)"), PRE * g + r, x1n_kept)

            def choose(g):
                for r in range(PRE):
                    b = PRE * g + r
                    dve.wait_ge(lg_done, 2 + b + 1)
                    lg = lg_p[r]
                    settled(dve)
                    st.after(V.max(top[:, r, :], lg))
                    settled(dve)
                    V.max_index(topi[:, r, :], top[:, r, :], lg).then_inc(lg_used, 1)
                dve.wait_ge(lg_used, 1 + PRE * (g + 1))
                V.tensor_copy(blk[:, ds(PRE * g, PRE)], topi[:, :, 0]).then_inc(chosen, 1)
            norms(0)
            with dve.Fori(0, NB // PRE - 1) as g:
                def both(g):
                    norms(g + 1)
                    choose(g)
                st.loop(g, 0, NB // PRE - 1, PRE, both)
            choose(NB // PRE - 1)
            dve.wait_ge(chosen, NB // PRE)

            def rows():
                V.tensor_copy(rows_i[:, 0:NB], pos[:, 0:NB]).then_inc(tok_rows, 1)
            for part_of_it in ranking(blk[:, 0:NB], NB, EXPERTS, CHUNKS, rows, ones[:, 0:EXPERTS], float(EXPERTS - 1),
                                      table[0:1, CHUNKS, :]):
                part_of_it()

            def step(t, r):
                fixed = isinstance(t, int)
                j = t - 1
                if not (fixed and (j < 0 or j >= XT)):
                    dve.wait_ge(hid_done, j + 1)
                    if not (fixed and j < 2):
                        dve.wait_ge(ht_done, j - 1)
                    V.tensor_scalar(hid[:, (r + 1) % 2, :], hid_p[(r + 1) % 2], 0.0, None, ALU.max).then_inc(hid_ready, 1)
                j, r = t - 3, (r + 1) % RING
                if not (fixed and (j < 0 or j >= XT)):
                    dve.wait_ge(o_done, j + 1)
                    if not (fixed and j < RING):
                        dve.wait_ge(stored[r], 4 * (j - r))
                    V.tensor_scalar(tok_res[:, r, :], res_p[r % 2], 0.0, None, ALU.max).then_inc(o_ready, 1)
            expert_steps(dve, step)
            for b in range(NB):
                dve.wait_ge(gathered[b // 5], 16 * 5)
                V.tensor_tensor(xs[:, b, :], xs[:, b, :], x1n[:, b, :], ALU.add).then_inc(y_ready, 1)

        @block.tensor
        def _(pe):
            T = nc.tensor

            def rank_sums(c, w):
                pe.wait_ge(cnt_ready, c + 1)
                T.matmul(before_p[:, 0:w], before[:, :], cnt[:, 0:w], start=True, stop=True)
                T.matmul(total_p[:, 0:w], ones[:, :], cnt[:, 0:w], start=True, stop=True).then_inc(cnt_sum, 1)

            def rank_row(c):
                pe.wait_ge(off_ready, c + 1)
                T.matmul(table_p, off[:, 0:1], ident[:, :], start=True, stop=True).then_inc(off_row, 1)

            def time_features(q):
                for h in range(2):
                    pe.wait_ge(attr_in[h], 32 * (q + 1))
                    pe.wait_ge(ring_ready[h], 1 + 3 * q)
                    for a in range(2):
                        T.matmul(tf_p[h][:, a * 3 * AD:(a + 1) * 3 * AD], attr_sb[:, h, a * P:(a + 1) * P], wt_sb[:, :],
                                 start=True, stop=True)
                    last = T.matmul(tf_p[h][:, 6 * AD:7 * AD], attr_sb[0:ED, h, 2 * P:3 * P], wt_sb[0:ED, 0:AD],
                                    start=True, stop=False)
                    last = T.matmul(tf_p[h][:, 6 * AD:7 * AD], ones[0:1, :], bt_sb[:, :], start=False, stop=True)
                    last.then_inc(tf_done[h], 1)

            def reduce_piece(c, i):
                pe.wait_ge(edges_in[i % 2], 16 * (PAIRS // 2 * c + i // 2 + 1))
                for r in range(GRPS):
                    t0 = i * PIECE + r * GRP
                    _, place = nc.values_load_multi_w_load_instructions(
                        table[0:1, ds(c, 1), t0:t0 + GRP].rearrange("a o t -> a (o t)"), engines=[mybir.EngineType.PE],
                        min_val=0, max_val=3 * BANK + 4 * SLOT,
                        skip_runtime_bounds_check_because="a sum of slot widths up to the spare slot")
                    pe.wait_ge(oh_ready[r], c * PAIRS + i + 1)
                    for j in range(GRP):
                        a = (r * GRP + j) * ROW
                        last = T.matmul(sums[:, ds(place[j], AD + 1)], node_oh[:, r, j * P:(j + 1) * P],
                                        edges_sb[:, i % 2, a:a + AD + 1], start=False, stop=True, skip_group_check=True)
                    last.then_inc(oh_used[r], 1)

            pe.wait_ge(consts, 5)
            pe.wait_ge(ones_set, 1)
            pe.wait_ge(gw_in, 16 * 7)
            rank_sums(0, NB)
            rank_row(0)
            time_features(0)
            rank_sums(1, NB)
            rank_row(1)
            pe.wait_ge(mw_in, 32)

            def transpose_norm(r, to, ready, done):
                for k in range(2):
                    last = T.transpose(to[:, k * P:(k + 1) * P], nrm[:, r, k * P:(k + 1) * P], ident[:, :])
                last.then_inc(done, 1)

            def prepare(b, r):
                pe.wait_ge(xn_ready, b + 1)
                pe.wait_ge(tr_copied, 1 + b)
                transpose_norm(r, trp, xn_ready, tr_done)
                pe.wait_ge(tr_copied, 1 + b + 1)
                pe.wait_ge(nf_ready, 1 + b)
                for k in range(2):
                    last = T.matmul(nf_p, wd_sb[:, k, :], xT[:, 0, k * P:(k + 1) * P], start=(k == 0), stop=(k == 1))
                last.then_inc(nf_done, 1)

            for r in range(PRE):
                prepare(r, r)
            with pe.Fori(1, PAIRS) as i:
                time_features(i)
                for r in range(PRE):
                    prepare(i * PRE + r, r)
            for b in range(PAIRS * PRE, NB):
                prepare(b, b % PRE)
            pe.wait_ge(nf_ready, 1 + NB)
            for k in range(4):
                T.matmul(slots[:, k, :], zrow[:, 0:P], zrow, start=True, stop=True)

            def stage(s, ranks=True):
                for i in range(PAIRS):
                    time_features(s * PAIRS + i)
                    if i == 0:
                        pe.wait_ge(table_ready, s)
                    if i == 2 and ranks:
                        rank_row(s + 1)
                    reduce_piece(s - 1, i)
                    if i == 0 and ranks:
                        rank_sums(s + 1, NB)

            with pe.Fori(1, CHUNKS - 1) as s:
                stage(s)
            stage(CHUNKS - 1, ranks=False)
            pe.wait_ge(table_ready, CHUNKS)
            for i in range(PAIRS):
                reduce_piece(CHUNKS - 1, i)

            pe.wait_ge(late_in, 16 * LATE)
            def mean_rows(g):
                pe.wait_ge(mean_ready, g + 1)
                for r in range(PRE):
                    to = tf_p[r // 4][:, r % 4 * P:(r % 4 + 1) * P]
                    last = T.transpose(to, mean5[:, r, :], ident[:, :])
                last.then_inc(mt_done, 1)

            def fuse(g):
                pe.wait_ge(mt_copied, 2 * g + 2)
                pe.wait_ge(fu_ready, 1 + 2 * g)
                for k in range(2):
                    last = T.matmul(fused_p[k], wf_sb[:, :], combT[:, ds(g * (PRE * P) + k * HALF, HALF)], start=True, stop=True)
                last.then_inc(fu_done, 1)

            def up(g):
                pe.wait_ge(fu_ready, 1 + 2 * g + 2)
                for r in range(PRE):
                    if r in (0, 4):
                        pe.wait_ge(x1_ready, 1 + PRE * g + r // 4)
                    T.matmul(up_p[r], fT[:, r * P:(r + 1) * P], wu_sb[:, :], start=True, stop=True).then_inc(up_done, 1)
            mean_rows(0)
            with pe.Fori(0, NG - 1) as g:
                fuse(g)
                mean_rows(g + 1)
                up(g)
            fuse(NG - 1)
            up(NG - 1)
            pe.wait_ge(x1_ready, 1 + NB)

            def norm_rows(b, r):
                pe.wait_ge(x1n_ready, b + 1)
                if not (isinstance(b, int) and b == 0):
                    pe.wait_ge(rt_copied, b)
                transpose_norm(r, rt_p[r % 3], x1n_ready, rt_done)

            def logits(b, r, g):
                pe.wait_ge(rt_copied, 1 + b + 1)
                pe.wait_ge(lg_used, 1 + PRE * g)
                for k in range(2):
                    T.matmul(lg_p[r], xT[:, r % 3, k * P:(k + 1) * P], rw_sb[:, k, :], start=(k == 0), stop=False)
                T.matmul(lg_p[r], ones[0:1, :], rb_sb[:, :], start=False, stop=True).then_inc(lg_done, 1)
            norm_rows(0, 0)
            with pe.Fori(0, NG - 1) as g:
                for r in range(PRE):
                    norm_rows(PRE * g + r + 1, (r + 1) % PRE)
                    logits(PRE * g + r, r, g)
            for r in range(PRE):
                if r < PRE - 1:
                    norm_rows(NB - PRE + r + 1, r + 1)
                logits(NB - PRE + r, r, NG - 1)
            rank_sums(CHUNKS, EXPERTS)
            rank_row(CHUNKS)
            pe.wait_ge(table_ready, CHUNKS + 1)

            def tile_experts(t):
                fixed = isinstance(t, int)
                first = max(0, t - 3) if fixed else t - 3
                n = min(6, XT - first) if fixed and t >= XT else 6
                _, e = nc.values_load_multi_w_load_instructions(
                    table[0:1, CHUNKS, ds(first, n)], engines=[mybir.EngineType.PE], min_val=0, max_val=EXPERTS - 1,
                    skip_runtime_bounds_check_because="clamped to the last expert")
                lead = t - first if fixed else 3
                return {k - lead: v for k, v in enumerate(e)}

            def step(t, r, expert):
                fixed = isinstance(t, int)
                h, o = r % 2, (r + 1) % 2
                if not (fixed and t >= XT):
                    pe.wait_ge(tok_loaded[r], 4 * (t - r) + 16)
                    if not (fixed and t < 2):
                        pe.wait_ge(tok_trc, t - 1)
                    for k in range(2):
                        last = T.transpose(tok_p[h][:, k * P:(k + 1) * P], tok_in[:, r, k * P:(k + 1) * P], ident[:, :])
                    last.then_inc(tok_tr, 1)
                j = t - 1
                if not (fixed and (j < 0 or j >= XT)):
                    e = expert[r - 1]
                    pe.wait_ge(tok_trc, j + 1)
                    if not (fixed and j < 2):
                        pe.wait_ge(hid_ready, j - 1)
                    for k in range(2):
                        T.matmul(hid_p[o], xT[:, o, k * P:(k + 1) * P], w1_sb[:, ds(e * (2 * AD) + k * AD, AD)],
                                 start=(k == 0), stop=False)
                    T.matmul(hid_p[o], ones[0:1, :], b1_sb[:, ds(e * AD, AD)], start=False, stop=True).then_inc(hid_done, 1)
                j = t - 2
                if not (fixed and (j < 0 or j >= XT)):
                    pe.wait_ge(hid_ready, j + 1)
                    if not (fixed and j < 2):
                        pe.wait_ge(ht_ready, j - 1)
                    settled(pe)
                    T.transpose(hT_p[h], hid[:, h, :], ident[:, :]).then_inc(ht_done, 1)
                j = t - 3
                if not (fixed and (j < 0 or j >= XT)):
                    e = expert[r - 3]
                    pe.wait_ge(ht_ready, j + 1)
                    if not (fixed and j < 2):
                        pe.wait_ge(o_ready, j - 1)
                    T.matmul(res_p[o], fT[:, o * P:(o + 1) * P], w2_sb[:, ds(e * CH, CH)], start=True, stop=True
                             ).then_inc(o_done, 1)
            expert_steps(pe, step, tile_experts)


_ARGS = ["x", "src", "attr_3", "attr_1", "wd_t", "bd", "wt_t", "bt", "wf_t", "bf", "wu_t", "bu", "rw_t", "rb", "w1", "b1", "w2", "b2"]


def kernel(**inputs):
    import concourse.bacc as bacc
    from concourse.bass_utils import run_bass_kernel_spmd

    a = {k: np.ascontiguousarray(v) for k, v in inputs.items()}
    c = np.ascontiguousarray
    x = np.zeros((NB * P, CH), a["x"].dtype)
    x[:NODES] = a["x"]
    src = np.full((ET * P,), NB * P - 1, a["src"].dtype)
    src[:EDGES] = a["src"]
    attr = np.zeros((ET * P, ED), a["edge_attr_32"].dtype)
    attr[:EDGES] = a["edge_attr_32"]
    attr = attr.reshape(P, ET // BATCH, BATCH, ED).transpose(1, 2, 3, 0)
    attr_3 = c(attr[:, 0:6].reshape(ET // BATCH, 2, 3 * ED, P).transpose(2, 0, 1, 3)).reshape(3 * ED, ET // BATCH * 2 * P)
    attr_1 = c(attr[:, 6].transpose(1, 0, 2)).reshape(ED, ET // BATCH * P)
    arrays = {
        "x": x, "src": src,
        "attr_3": attr_3, "attr_1": attr_1,
        "wd_t": c(a["L0_gnn_W_down"].T), "bd": a["L0_gnn_b_down"].reshape(AD, 1),
        "wt_t": c(a["L0_gnn_W_time"].T), "bt": a["L0_gnn_b_time"].reshape(1, AD),
        "wf_t": c(a["L0_gnn_W_fusion"].T), "bf": a["L0_gnn_b_fusion"].reshape(AD, 1),
        "wu_t": c(a["L0_gnn_W_up"].T), "bu": a["L0_gnn_b_up"].reshape(1, CH),
        "rw_t": c(a["L0_ffn_router_w"].T), "rb": a["L0_ffn_router_b"].reshape(1, EXPERTS),
        "w1": c(a["L0_ffn_W1"].reshape(EXPERTS, 2, P, AD).transpose(2, 0, 1, 3)).reshape(P, EXPERTS * 2 * AD),
        "b1": a["L0_ffn_b1"].reshape(1, EXPERTS * AD),
        "w2": c(a["L0_ffn_W2"].transpose(1, 0, 2)).reshape(AD, EXPERTS * CH), "b2": a["L0_ffn_b2"].reshape(1, EXPERTS * CH),
    }
    nc = bacc.Bacc("TRN2", target_bir_lowering=False, num_devices=1)
    maps, aps = {}, []
    for name in _ARGS:
        maps[f"{name}_dram"] = arrays[name]
        aps.append(nc.dram_tensor(f"{name}_dram", arrays[name].shape, mybir.dt.from_np(arrays[name].dtype),
                                  kind="ExternalInput").ap())
    out = nc.dram_tensor("out_dram", (NODES, CH), f32, kind="ExternalOutput").ap()
    program(nc, *aps, out)
    r = run_bass_kernel_spmd(nc, [maps], core_ids=[0])
    return r.results[0]["out_dram"]
```

```python
from contextlib import ExitStack

import numpy as np
import concourse.bass as bass
from concourse import mybir

P = 128
NODES, CH, EDGES, ED = 3125, 256, 50000, 32
AD = 64
EXPERTS = 32
NB = -(-NODES // P)
CHUNKS, PAIRS, BATCH = 7, 4, 7
CT = PAIRS * 2 * BATCH
ET = CHUNKS * CT
GRP, GRPS = 4, 5
PIECE = GRPS * GRP
ST = PAIRS * PIECE
assert ET * P >= EDGES and ST >= CT + NB - 1 and ST <= P
ROW = AD + 2
PER_BANK, SLOT = 7, 72
BANK = 512
XT = NB + EXPERTS - 1
PRE = 5
NG = NB // PRE
PRE_HALVES = range(0, 2), range(2, PRE)
assert NB % PRE == 0
UP = AD + EXPERTS + 1
RING = 8
TROW = CH + 2
NO_NODE = NB * P - 1
assert NO_NODE >= NODES
EPS = 1e-5

f32, bf16, i32, u32 = mybir.dt.float32, mybir.dt.bfloat16, mybir.dt.int32, mybir.dt.uint32
ALU, ACT = mybir.AluOpType, mybir.ActivationFunctionType
AXX = mybir.AxisListType.X
ds = bass.ds


class Count:

    def __init__(self, eng, sem):
        self.eng, self.sem, self.n = eng, sem, 0

    def after(self, ins):
        ins.then_inc(self.sem, 1)
        self.n = self.n + 1
        self.eng.wait_ge(self.sem, self.n)

    def loop(self, i, start, stop, steps, body):
        n0 = self.n
        self.n = n0 + (i - start) * steps
        body(i)
        self.n = n0 + (stop - start) * steps


def program(nc, x, src, attr_3, attr_1, wd_t, bd, wt_t, bt, wf_t, bf, wu_t, bu, wu_b, rw_t, rb, w1, b1, w2, b2, out):
    ctx = ExitStack()
    with ctx:
        def sb(name, shape, dt=f32):
            return ctx.enter_context(nc.sbuf_tensor(name, shape, dt))

        def sem(name):
            return ctx.enter_context(nc.semaphore(name))

        edges_sorted = nc.dram_tensor("edges_sorted", (CHUNKS * P * ST, ROW), f32, kind="Internal").ap()
        tokens = nc.dram_tensor("tokens", (NB * P, TROW), f32, kind="Internal").ap()

        table = sb("table", [1, CHUNKS + 1, P], i32)
        ident = sb("ident", [P, P])
        ones = sb("ones", [P, P])
        before = sb("before", [P, P])
        iota_i = sb("iota_i", [P, P], i32)
        iota = sb("iota", [P, P])
        part_i = sb("part_i", [P, 1], i32)
        part = sb("part", [P, 1])
        slot_w = sb("slot_w", [P, NB])
        empty_row = sb("empty_row", [P, PIECE * ROW])
        zrow = sb("zrow", [1, BANK], bf16)
        blocks_left = sb("blocks_left", [P, NB])
        parts_left = sb("parts_left", [P, 1])
        epsb = sb("epsb", [P, 1])
        chunk_base = sb("chunk_base", [P, CHUNKS])

        src_i = sb("src_i", [P, ET], i32)
        tmp_i = sb("tmp_i", [P, ET], i32)
        blk = sb("blk", [P, ET])
        lo = sb("lo", [P, ET])
        rows_i = sb("rows_i", [P, ET], i32)
        onehot = sb("onehot", [P, NB, CT], bf16)
        cum = sb("cum", [P, NB, CT])
        pos = sb("pos", [P, CT])
        pos_i = sb("pos_i", [P, CT], i32)
        pos_h = sb("pos_h", [P, CT], i32)
        pos_l = sb("pos_l", [P, CT], i32)
        cend = sb("cend", [P, EXPERTS + 1])
        cnt = sb("cnt", [P, EXPERTS])
        nt_i = sb("nt_i", [P, EXPERTS], i32)
        nt = sb("nt", [P, EXPERTS])
        tend = sb("tend", [P, EXPERTS])
        base = sb("base", [P, EXPERTS])
        le = sb("le", [P, EXPERTS])
        off = sb("off", [P, 1])

        attr_sb = sb("attr_sb", [3 * ED + 1, 2, 3 * P])
        ring = sb("ring", [P, 2, BATCH * ROW])
        idx_ring = sb("idx_ring", [P, 2, BATCH], u32)
        edges_sb = sb("edges_sb", [P, 2, PIECE * ROW])
        onehots = sb("onehots", [P, PIECE * P])
        node_oh = onehots[:, :].bitcast(bf16).rearrange("p (h r n) -> p h r n", h=2, r=GRPS)
        split = [sb(f"split{k}", [P, 2, PIECE * w], bf16) for k, w in enumerate((AD + 1, AD, AD))]

        wd_sb = sb("wd_sb", [P, 2, AD + EXPERTS])
        bd_sb = sb("bd_sb", [AD, 1])
        wt_sb = sb("wt_sb", [3 * ED + 1, 3 * AD])
        wt1_sb = sb("wt1_sb", [ED + 1, AD])
        wf_sb = sb("wf_sb", [P, AD])
        bf_sb = sb("bf_sb", [AD, 1])
        wu_sb = sb("wu_sb", [UP, CH + 2 * EXPERTS])
        wub_sb = sb("wub_sb", [P, 2, UP])
        rw_sb = sb("rw_sb", [P, 2, EXPERTS])
        rwc = wd_sb[:, :, AD:AD + EXPERTS]
        rb_sb = sb("rb_sb", [P, EXPERTS])
        b1_sb = sb("b1_sb", [P, EXPERTS * AD])
        w1_sb = sb("w1_sb", [P, EXPERTS * 2 * AD])
        w2_sb = sb("w2_sb", [AD + 1, EXPERTS * CH])

        token = sb("token", [P, NB, TROW])
        xs = token[:, :, 0:CH]
        nrm = sb("nrm", [P, PRE, CH])
        tmean = edges_sb[:, :, :].rearrange("p h n -> p (h n)")[:, 0:NB * AD]
        combT = sb("combT", [P, NB * P])
        stats = sb("stats", [P, PRE, 6])
        mv5 = sb("mv5", [P, PRE, 2])
        mv = sb("mv", [P, NB, 2])
        rstd = sb("rstd", [P, NB])
        gain = sb("gain", [P, NB])
        rcount = sb("rcount", [P, NB])
        xT = sb("xT", [P, 3, 2 * P])
        lgT_all = sb("lgT_all", [P, NB * P])
        lgT = lgT_all[0:AD + EXPERTS, :]
        fT = sb("fT", [UP, PRE * P])
        hT = sb("hT", [AD + 1, 2 * P])
        parts = sb("parts", [P, NB, 2 * EXPERTS])
        top = sb("top", [P, NB])
        from_last = sb("from_last", [P, EXPERTS])
        hid = sb("hid", [P, 2, AD])
        tok_in = onehots[:, 0:RING * TROW].rearrange("p (r c) -> p r c", r=RING)
        place_oh = combT[:, 0:NB * P // 2].bitcast(bf16)
        tok_res = combT[:, 0:RING * CH].rearrange("p (r c) -> p r c", r=RING)
        lefts = lgT_all[:, 0:NB * XT].bitcast(bf16).rearrange("p (b k t) -> p b k t", b=NB, k=2)
        perm = sb("perm", [P, XT], u32)
        perm_f = sb("perm_f", [P, XT])

        sums = ctx.enter_context(nc.psum_tensor("sums", [P, 4 * BANK], f32))
        tfp = ctx.enter_context(nc.psum_tensor("tfp", [P, 2 * BANK], f32))
        trp = ctx.enter_context(nc.psum_tensor("trp", [P, BANK], f32))
        mmp = ctx.enter_context(nc.psum_tensor("mmp", [P, BANK], f32))
        banks = [sums[:, k * BANK:(k + 1) * BANK] for k in range(4)]
        tf_p = [tfp[:, h * BANK:(h + 1) * BANK] for h in range(2)]
        HALF = PRE * P // 2
        fused_p = [mmp[0:AD, 0:HALF], trp[0:AD, 0:HALF]]
        up_p = [b[:, 0:CH + 2 * EXPERTS] for b in banks] + [tf_p[1][:, P:P + CH + 2 * EXPERTS]]
        rw_sum, wur_p = banks[2][:, 0:EXPERTS], banks[3][0:UP, 0:EXPERTS]
        perm_p = trp[:, 0:2 * XT]
        nf_p = banks[0][0:AD + EXPERTS, 0:P]
        tok_p = [b[:, 0:2 * P] for b in tf_p]
        hid_p = [b[:, 0:AD] for b in (mmp, trp)]
        hT_p = [b[0:AD, 0:P] for b in banks[2:4]]
        res_p = [b[:, 0:CH] for b in banks[0:2]]
        slots = sums[:, :].rearrange("p (k c) -> p k c", k=4)
        before_p, total_p, table_p = mmp[:, 0:EXPERTS], mmp[:, 64:64 + EXPERTS], mmp[0:1, 128:256]

        consts = sem("consts")
        ones_set = sem("ones_set")
        empty_set = sem("empty_set")
        rows_set = sem("rows_set")
        src_in, x_in, gw_in, mw_in, late_in = sem("src_in"), sem("x_in"), sem("gw_in"), sem("mw_in"), sem("late_in")
        cleared = sem("cleared")
        wt_zero, wu_zero = sem("wt_zero"), sem("wu_zero")
        attr_in = [sem(f"attr_in{h}") for h in range(2)]
        tf_done = [sem(f"tf_done{h}") for h in range(2)]
        ring_ready = [sem(f"ring_ready{h}") for h in range(2)]
        scattered = [sem(f"scattered{h}") for h in range(2)]
        edges_in = [sem(f"edges_in{h}") for h in range(2)]
        oh_ready = [sem(f"oh_ready{r}") for r in range(GRPS)]
        oh_used = [sem(f"oh_used{r}") for r in range(GRPS)]
        part_ready = [sem(f"part_ready{k}") for k in range(3)]
        last_part = [sem(f"last_part{k}") for k in range(2)]
        left_ready = sem("left_ready")
        dve_step, pool_step = sem("dve_step"), sem("pool_step")
        cnt_ready, cnt_sum, off_ready, off_row, table_ready, rows_ready = (
            sem("cnt_ready"), sem("cnt_sum"), sem("off_ready"), sem("off_row"), sem("table_ready"), sem("rows_ready"))
        var_ready, std_ready, xn_ready = sem("var_ready"), sem("std_ready"), sem("xn_ready")
        tr_done, tr_copied, nf_done, nf_ready = sem("tr_done"), sem("tr_copied"), sem("nf_done"), sem("nf_ready")
        mean_ready, mt_done, mt_copied, fu_done, fu_ready, up_done, x1_ready = (
            sem("mean_ready"), sem("mt_done"), sem("mt_copied"), sem("fu_done"), sem("fu_ready"), sem("up_done"), sem("x1_ready"))
        tok_built, tok_normed, tok_out = sem("tok_built"), sem("tok_normed"), sem("tok_out")
        rw_summed, rwc_ready, wur_done, wur_ready = sem("rw_summed"), sem("rwc_ready"), sem("wur_done"), sem("wur_ready")
        lg_kept, lg_ready, lg_scaled, lg_whole, rstd_ready = (
            sem("lg_kept"), sem("lg_ready"), sem("lg_scaled"), sem("lg_whole"), sem("rstd_ready"))
        oh_built, perm_summed, perm_ready = sem("oh_built"), sem("perm_summed"), sem("perm_ready")
        tok_loaded = [sem(f"tok_loaded{h}") for h in range(RING)]
        tok_tr, tok_trc, hid_done, hid_ready, ht_done, ht_ready, o_done, o_ready = (
            sem("tok_tr"), sem("tok_trc"), sem("hid_done"), sem("hid_ready"), sem("ht_done"), sem("ht_ready"),
            sem("o_done"), sem("o_ready"))
        stored = [sem(f"stored{h}") for h in range(RING)]

        started = {f: 1 for f in (*ring_ready, tr_copied, nf_ready, tr_done, fu_ready, x1_ready, up_done,
                                  mt_done, lg_kept, lg_ready)}
        started |= {f: 2 for f in (*oh_used, part_ready[2])}

        def settled(eng):
            eng.sem_inc(passed[eng.engine], 1)

        passed = {eng.engine: sem(f"passed_{name}") for name, eng in
                  (("dve", nc.vector), ("pool", nc.gpsimd), ("pe", nc.tensor))}

        def expert_steps(eng, step, group=None, after=3):
            def steps(t, n=RING):
                for r in range(n):
                    if r % 4 == 0:
                        values = (group(t + r),) if group else ()
                    step(t + r, r, *values)
            steps(0)
            steps(RING)
            with eng.Fori(2, XT // RING) as m:
                steps(m * RING)
            steps(XT, after)

        AHEAD = 3

        def due(s, i):
            return not isinstance(s, int) or 2 * PAIRS <= s * PAIRS + i + AHEAD < PAIRS * CHUNKS

        def group_logits(g):
            blocks = ds(PRE * g, PRE)
            return (blocks, parts[:, blocks, EXPERTS:2 * EXPERTS],
                    lambda a: a[:, blocks].rearrange("p (b o) -> p b o", o=1).to_broadcast([P, PRE, EXPERTS]),
                    lambda a: a[:, :].rearrange("p (o e) -> p o e", o=1).to_broadcast([P, PRE, EXPERTS]))

        def piece_parts(i):
            rows = edges_sb[:, i % 2, :].rearrange("p (j f) -> p j f", f=ROW)
            return rows, rows[:, :, 0:AD], [part[:, i % 2, :].rearrange("p (j f) -> p j f", j=PIECE) for part in split]

        def piece_is_in(eng, c, i):
            eng.wait_ge(edges_in[i % 2], 16 * (PAIRS // 2 * c + i // 2 + 1))
            eng.wait_ge(oh_used[-1], 1 + PAIRS * c + i)

        LATE = 4 + 4 * 3
        block = ctx.enter_context(nc.Block())

        @block.sync
        def _(sp):
            sp.dma_start(src_i[:, :], src.rearrange("(p t) -> p t", p=P)).then_inc(src_in, 16)
            def clear(c, i):
                dst = edges_sorted[:, :].rearrange("(c p j) f -> c p (j f)", c=CHUNKS, p=P)
                sp.dma_start(dst[ds(c, 1), :, i * PIECE * ROW:(i + 1) * PIECE * ROW].rearrange("o p n -> (o p) n"),
                             empty_row[:, :]).then_inc(cleared, 16)

            def attributes(q, first=False):
                for h in range(2):
                    if not first:
                        sp.wait_ge(tf_done[h], q)
                    sp.dma_start(attr_sb[0:3 * ED, h, 0:2 * P], attr_3[:, ds((2 * q + h) * 2 * P, 2 * P)]).then_inc(attr_in[h], 16)
                    sp.dma_start(attr_sb[0:ED, h, 2 * P:3 * P], attr_1[:, ds((2 * q + h) * P, P)]).then_inc(attr_in[h], 16)

            def load_piece(c, i):
                if i == 0:
                    for h in range(2):
                        sp.wait_ge(scattered[h], BATCH * 16 * PAIRS * (c + 1))
                sp.wait_ge(part_ready[2], 1 + PAIRS * c + i)
                sp.dma_start(edges_sb[:, i % 2, :], edges_sorted[:, :].rearrange("(c p j) f -> c p (j f)", c=CHUNKS, p=P)
                             [ds(c, 1), :, i * PIECE * ROW:(i + 1) * PIECE * ROW].rearrange("o p n -> (o p) n")
                             ).then_inc(edges_in[i % 2], 16)

            attributes(0, first=True)
            sp.wait_ge(wt_zero, 1)
            sp.wait_ge(empty_set, 1)
            for i in range(PAIRS):
                clear(0, i)
            for k in range(3):
                sp.dma_start(wt_sb[k * ED:(k + 1) * ED, k * AD:(k + 1) * AD], wt_t).then_inc(gw_in, 16)
                sp.dma_start(wt_sb[3 * ED:3 * ED + 1, k * AD:(k + 1) * AD], bt).then_inc(gw_in, 16)
            sp.dma_start(wt1_sb[0:ED, :], wt_t).then_inc(gw_in, 16)
            sp.dma_start(wt1_sb[ED:ED + 1, :], bt).then_inc(gw_in, 16)
            sp.dma_start(xs[:, :, :], x.rearrange("(b p) c -> p b c", p=P)).then_inc(x_in, 16)
            sp.dma_start(wd_sb[:, :, 0:AD], wd_t.rearrange("(k p) n -> p k n", p=P)).then_inc(mw_in, 16)
            sp.dma_start(bd_sb[:, :], bd).then_inc(mw_in, 16)
            sp.dma_start(rw_sb[:, :, :], rw_t.rearrange("(k p) n -> p k n", p=P)).then_inc(mw_in, 16)
            sp.dma_start(wub_sb[:, :, :], wu_b.rearrange("(k p) n -> p k n", p=P)).then_inc(mw_in, 16)
            sp.wait_ge(wu_zero, 1)
            sp.dma_start(wu_sb[0:AD, 0:CH], wu_t).then_inc(mw_in, 16)
            sp.dma_start(wu_sb[UP - 1:UP, 0:CH], bu).then_inc(mw_in, 16)
            sp.wait_ge(cleared, 16 * PAIRS)
            for i in range(PAIRS):
                attributes(i + 1)
                clear(1, i)
            sp.wait_ge(cleared, 2 * 16 * PAIRS)
            for i in range(PAIRS):
                if i > 0:
                    attributes(PAIRS + i)
                clear(2, i)
            sp.dma_start(wf_sb[:, :], wf_t).then_inc(late_in, 16)
            sp.dma_start(bf_sb[:, :], bf).then_inc(late_in, 16)
            sp.dma_start(rb_sb[:, :], rb.to_broadcast([P, EXPERTS])).then_inc(late_in, 16)
            sp.dma_start(b1_sb[:, :], b1.to_broadcast([P, EXPERTS * AD])).then_inc(late_in, 16)

            def stage(s, ahead=None):
                for i in range(PAIRS):
                    if due(s, i):
                        attributes(PAIRS * s + i + AHEAD)
                    if ahead:
                        ahead(s, i)
                    if i == 0:
                        load_piece(s - 1, 0)
                        load_piece(s - 1, 1)
                    elif i < PAIRS - 1:
                        load_piece(s - 1, i + 1)

            def clear_next(s, i):
                if i == 0:
                    sp.wait_ge(cleared, 16 * PAIRS * (s + 2))
                clear(s + 2, i)

            def share(s, i):
                clear_next(s, i)
                if i == 0:
                    n = EXPERTS // 4 * 2 * AD
                    sp.dma_start(w1_sb[:, ds((s - 1) * n, n)], w1[:, ds((s - 1) * n, n)]).then_inc(late_in, 16)
                elif i == 1:
                    n = EXPERTS // 4 * CH
                    sp.dma_start(w2_sb[0:AD, ds((s - 1) * n, n)], w2[:, ds((s - 1) * n, n)]).then_inc(late_in, 16)
                    sp.dma_start(w2_sb[AD:AD + 1, ds((s - 1) * n, n)], b2[:, ds((s - 1) * n, n)]).then_inc(late_in, 16)

            stage(1, share)
            with sp.Fori(2, CHUNKS - 2) as s:
                stage(s, share)
            stage(CHUNKS - 2)
            stage(CHUNKS - 1)
            for i in range(PAIRS):
                load_piece(CHUNKS - 1, i)

            with sp.Fori(0, NG) as g:
                sp.wait_ge(tok_built, 2 * (g + 1))
                sp.wait_ge(x1_ready, 1 + PRE * (g + 1))
                sp.dma_start(tokens[ds(g * (PRE * P), PRE * P), :].rearrange("(b p) c -> p b c", p=P),
                             token[:, ds(g * PRE, PRE), :]).then_inc(tok_out, 16)

        @block.gpsimd
        def _(pool):
            for freed, n in started.items():
                pool.sem_inc(freed, n)
            pool.iota(iota_i[:, :], pattern=[[1, P]], base=0, channel_multiplier=0).then_inc(consts, 1)
            pool.iota(part_i[:, :], pattern=[[1, 1]], base=0, channel_multiplier=1).then_inc(consts, 1)
            pool.memset(ident[:, :], 0.0).then_inc(pool_step, 1)
            pool.memset(before[:, :], 0.0).then_inc(pool_step, 1)
            pool.wait_ge(pool_step, 2)
            pool.affine_select(out=before[:, :], in_=before[:, :], compare_op=ALU.is_ge, fill=1.0,
                               base=0, pattern=[[-1, P]], channel_multiplier=1).then_inc(consts, 1)
            pool.affine_select(out=ident[:, :], in_=ident[:, :], compare_op=ALU.not_equal, fill=1.0,
                               base=0, pattern=[[-1, P]], channel_multiplier=1).then_inc(consts, 1)
            empty_rows = empty_row[:, :].rearrange("p (j f) -> p j f", f=ROW)
            pool.memset(empty_rows[:, :, 0:ROW - 1], 0.0).then_inc(pool_step, 1)
            pool.wait_ge(pool_step, 3)
            pool.memset(empty_rows[:, :, ROW - 1:ROW], -1.0).then_inc(empty_set, 1)
            pool.wait_ge(empty_set, 1)
            pool.memset(wu_sb[:, :], 0.0).then_inc(wu_zero, 1)
            pool.wait_ge(wu_zero, 1)
            for n, (row, value) in enumerate(((attr_sb[3 * ED:3 * ED + 1, :, 0:2 * P], 1.0), (attr_sb[ED:ED + 1, :, 2 * P:3 * P], 1.0),
                                              (zrow[:, :], 0.0), (fT[UP - 1:UP, :], 1.0), (hT[AD:AD + 1, :], 1.0))):
                pool.memset(row, value).then_inc(rows_set, 1)
                pool.wait_ge(rows_set, n + 1)

            with pool.Fori(0, CHUNKS) as s:
                pool.wait_ge(cleared, 16 * PAIRS * (s + 1))
                settled(pool)
                with pool.Fori(0, PAIRS) as i:
                    for h in range(2):
                        pool.wait_ge(ring_ready[h], 1 + 3 * (PAIRS * s + i + 1))
                        settled(pool)
                        for j in range(BATCH):
                            pool.indirect_dma_start(
                                edges_sorted[:, :], bass.IndirectOffsetOnAxis(ap=idx_ring[:, h, j:j + 1], axis=0),
                                ring[:, h, j * ROW:(j + 1) * ROW], None).then_inc(scattered[h], 16)

            pool.wait_ge(late_in, 16 * LATE)
            with pool.Fori(0, NG) as g:
                blocks, lg, by_block, by_expert = group_logits(g)
                def on(ins, done, n):
                    ins.then_inc(done, 1)
                    pool.wait_ge(done, n)
                    settled(pool)
                pool.wait_ge(lg_ready, 1 + PRE * (g + 1))
                settled(pool)
                on(nc.gpsimd.tensor_tensor(lg, lg, by_block(gain), ALU.mult), lg_scaled, 3 * g + 1)
                on(nc.gpsimd.tensor_tensor(lg, lg, parts[:, blocks, 0:EXPERTS], ALU.add), lg_scaled, 3 * g + 2)
                pool.wait_ge(rstd_ready, g + 1)
                settled(pool)
                on(nc.gpsimd.tensor_tensor(lg, lg, by_block(rstd), ALU.mult), lg_scaled, 3 * g + 3)
                on(nc.gpsimd.tensor_tensor(lg, lg, by_expert(rb_sb), ALU.add), lg_whole, g + 1)
                nc.gpsimd.tensor_copy(token[:, blocks, CH:CH + 1], mv[:, blocks, 0:1]).then_inc(tok_built, 1)
                pool.wait_ge(tok_built, 2 * g + 1)
                settled(pool)
                nc.gpsimd.tensor_copy(token[:, blocks, CH + 1:CH + 2], rstd[:, blocks].rearrange("p (b o) -> p b o", o=1)
                                      ).then_inc(tok_built, 1)
                pool.wait_ge(tok_built, 2 * g + 2)

            pool.wait_ge(perm_ready, 1)
            pool.wait_ge(tok_out, 16 * NG)
            def gather(t):
                pool.indirect_dma_start(tok_in[:, t % RING, :], None, tokens[:, :],
                                        bass.IndirectOffsetOnAxis(ap=perm[:, t:t + 1], axis=0)).then_inc(tok_loaded[t % RING], 16)
            for t in range(RING):
                gather(t)
            for t in range(XT):
                pool.wait_ge(o_ready, t + 1)
                if t + RING < XT:
                    gather(t + RING)
                pool.indirect_dma_start(out[:, :], bass.IndirectOffsetOnAxis(ap=perm[:, t:t + 1], axis=0),
                                        tok_res[:, t % RING, :], None, bounds_check=NODES - 1, oob_is_err=False
                                        ).then_inc(stored[t % RING], 16)
            for r in range(RING):
                pool.wait_ge(stored[r], 16 * (XT // RING))

        @block.scalar
        def _(act):
            def batches(q, first=False, between=lambda h: None):
                for h in range(2):
                    act.wait_ge(tf_done[h], q + 1)
                    if not first:
                        act.wait_ge(scattered[h], BATCH * 16 * q)
                    r = ring[:, h, :].rearrange("p (j f) -> p j f", f=ROW)
                    act.activation(r[:, :, 0:AD], tfp[:, h * BANK:h * BANK + BATCH * AD].rearrange("p (j f) -> p j f", f=AD),
                                   ACT.Relu).then_inc(ring_ready[h], 1)
                    if first:
                        act.wait_ge(rows_ready, 1)
                    act.activation(r[:, :, ROW - 1], lo[:, ds((2 * q + h) * BATCH, BATCH)], ACT.Copy).then_inc(ring_ready[h], 1)
                    act.activation(idx_ring[:, h, :], rows_i[:, ds((2 * q + h) * BATCH, BATCH)], ACT.Copy
                                   ).then_inc(ring_ready[h], 1)
                    between(h)

            def stdev(ready, blocks):
                act.wait_ge(var_ready, ready)
                act.activation(rstd[:, blocks], mv[:, blocks, 1], ACT.Sqrt, bias=epsb[:, 0:1]).then_inc(std_ready, 1)

            def stdev_x1(g):
                stdev(NG + g + 1, ds(g * PRE, PRE))

            act.wait_ge(ones_set, 1)
            def prepare_group(g):
                def norm(r):
                    act.wait_ge(tr_done, 1 + g * PRE + r + 1)
                    act.activation(xT[:, r % 3, :], trp[:, 0:2 * P], ACT.Copy).then_inc(tr_copied, 1)

                def features(r):
                    b = g * PRE + r
                    act.wait_ge(nf_done, b + 1)
                    act.activation(combT[0:AD, ds(b * P, P)], nf_p[0:AD, :], ACT.Relu, bias=bd_sb[:, 0:1]).then_inc(nf_ready, 1)
                    act.activation(lgT[AD:AD + EXPERTS, ds(b * P, P)], nf_p[AD:AD + EXPERTS, :], ACT.Copy).then_inc(lg_kept, 1)
                def half(h):
                    if h == 0:
                        norm(0)
                    for r in PRE_HALVES[h]:
                        if r + 1 < PRE:
                            norm(r + 1)
                        features(r)
                return half

            batches(0, first=True)
            batches(1)
            stdev(NG, slice(0, NB))
            act.wait_ge(mw_in, 16 * 6)
            with act.Fori(2, PAIRS) as i:
                batches(i, between=prepare_group(i - 2))
            act.wait_ge(rows_ready, 2)
            batches(PAIRS, between=prepare_group(2))
            batches(PAIRS + 1, between=prepare_group(3))
            batches(PAIRS + 2, between=prepare_group(4))
            batches(PAIRS + 3)
            act.wait_ge(rows_ready, 3)
            batches(2 * PAIRS)
            with act.Fori(2, CHUNKS - 1) as s:
                with act.Fori(0, PAIRS - 1) as i:
                    batches(PAIRS * s + i + 1)
                act.wait_ge(rows_ready, s + 2)
                batches(PAIRS * (s + 1))
            with act.Fori(PAIRS * (CHUNKS - 1) + 1, PAIRS * CHUNKS) as q:
                batches(q)

            for i in range(PAIRS):
                n = PAIRS * (CHUNKS - 1) + i
                rows, feats, into = piece_parts(i)
                piece_is_in(act, CHUNKS - 1, i)
                act.activation(into[0], rows[:, :, 0:AD + 1], ACT.Copy).then_inc(last_part[0], 1)
                act.wait_ge(left_ready, n + 1)
                act.activation(into[1], feats, ACT.Copy).then_inc(last_part[1], 1)

            act.wait_ge(late_in, 16 * LATE)
            act.wait_ge(lg_kept, 1 + NB)

            def means_transposed(g):
                act.wait_ge(mt_done, 1 + g + 1)
                act.activation(combT[AD:P, ds(g * PRE * P, 4 * P)], tf_p[0][0:AD, :], ACT.Copy).then_inc(mt_copied, 1)
                act.activation(combT[AD:P, ds((g * PRE + 4) * P, P)], tf_p[1][0:AD, 0:P], ACT.Copy).then_inc(mt_copied, 1)

            def fused(g):
                act.wait_ge(fu_done, g + 1)
                act.wait_ge(up_done, 1 + PRE * g)
                act.activation(fT[AD:AD + EXPERTS, :], lgT[AD:AD + EXPERTS, ds(g * (PRE * P), PRE * P)], ACT.Copy).then_inc(fu_ready, 1)
                for k, half in enumerate(fused_p):
                    act.activation(fT[0:AD, k * HALF:(k + 1) * HALF], half, ACT.Relu, bias=bf_sb[:, 0:1]).then_inc(fu_ready, 1)
            means_transposed(0)
            fused(0)
            means_transposed(1)
            with act.Fori(1, NG - 1) as g:
                fused(g)
                means_transposed(g + 1)
                stdev_x1(g - 1)
            fused(NG - 1)
            stdev_x1(NG - 2)
            stdev_x1(NG - 1)

            def step(t, r):
                h = r % 2
                if not (isinstance(t, int) and t >= XT):
                    act.wait_ge(tok_tr, t + 1)
                    if not (isinstance(t, int) and t < 2):
                        act.wait_ge(hid_done, t - 1)
                    act.activation(xT[:, h, :], tok_p[h], ACT.Copy).then_inc(tok_trc, 1)
                j = t - 2
                if not (isinstance(t, int) and (j < 0 or j >= XT)):
                    act.wait_ge(ht_done, j + 1)
                    if not (isinstance(t, int) and j < 2):
                        act.wait_ge(o_done, j - 1)
                    act.activation(hT[0:AD, h * P:(h + 1) * P], hT_p[h], ACT.Relu).then_inc(ht_ready, 1)
            expert_steps(act, step)

        @block.vector
        def _(dve):
            st = Count(dve, dve_step)
            V = nc.vector
            dve.wait_ge(consts, 2)
            V.memset(wt_sb[:, :], 0.0).then_inc(wt_zero, 1)
            V.memset(ones[:, :], 1.0).then_inc(dve_step, 1)
            V.memset(ring[:, :, :].rearrange("p h (j f) -> p h j f", f=ROW)[:, :, :, AD], 1.0).then_inc(dve_step, 1)
            V.memset(epsb[:, :], EPS).then_inc(dve_step, 1)
            V.memset(cend[:, 0:1], 0.0).then_inc(dve_step, 1)
            V.memset(slot_w[:, :], float(SLOT)).then_inc(dve_step, 1)
            V.tensor_copy(iota[:, :], iota_i[:, :]).then_inc(dve_step, 1)
            V.tensor_copy(part[:, :], part_i[:, :]).then_inc(dve_step, 1)
            st.n = 7
            dve.wait_ge(dve_step, st.n)
            V.memset(slot_w[:, PER_BANK - 1:NB:PER_BANK], float(BANK - (PER_BANK - 1) * SLOT)).then_inc(ones_set, 1)
            dve.wait_ge(ones_set, 1)
            V.tensor_scalar(blocks_left[:, :], iota[:, 0:NB], -1.0, float(NB - 1), ALU.mult, ALU.add).then_inc(ones_set, 1)
            V.tensor_scalar(parts_left[:, :], part[:, :], -1.0, float(P - 1), ALU.mult, ALU.add).then_inc(ones_set, 1)
            V.tensor_scalar(from_last[:, :], iota[:, 0:EXPERTS], -1.0, float(EXPERTS), ALU.mult, ALU.add).then_inc(ones_set, 1)
            dve.wait_ge(src_in, 16)
            st.after(V.tensor_scalar(tmp_i[:, :], src_i[:, :], 7, None, ALU.logical_shift_right))
            st.after(V.tensor_copy(blk[:, :], tmp_i[:, :]))
            st.after(V.tensor_scalar(tmp_i[:, :], src_i[:, :], P - 1, None, ALU.bitwise_and))
            st.after(V.tensor_copy(lo[:, :], tmp_i[:, :]))

            flat = lambda a: a.rearrange("p b t -> p (b t)")

            def ranking(key, n, w, c, row_of, weight, last, table_out):
                oh = flat(onehot[:, :, :])[:, 0:w * n].rearrange("p (b t) -> p b t", t=n)
                cu = flat(cum[:, :, :])[:, 0:w * n].rearrange("p (b t) -> p b t", t=n)

                def count():
                    st.after(V.tensor_tensor(oh, key.rearrange("p (o t) -> p o t", o=1).to_broadcast([P, w, n]),
                                             iota[:, 0:w].rearrange("p (b o) -> p b o", o=1).to_broadcast([P, w, n]),
                                             ALU.is_equal))
                    st.after(V.tensor_tensor_scan(flat(cu), ones[:, 0:1].to_broadcast([P, w * n]), flat(oh), 0.0,
                                                  ALU.mult, ALU.add))
                    st.after(V.tensor_copy(cend[:, 1:w + 1], cu[:, :, n - 1]))
                    V.tensor_tensor(cnt[:, 0:w], cend[:, 1:w + 1], cend[:, 0:w], ALU.subtract).then_inc(cnt_ready, 1)

                def place():
                    dve.wait_ge(cnt_sum, c + 1)
                    st.after(V.tensor_scalar(nt_i[:, 0:w], total_p[:, 0:w], float(P - 1), None, ALU.add))
                    st.after(V.tensor_scalar(nt_i[:, 0:w], nt_i[:, 0:w], 7, None, ALU.logical_shift_right))
                    st.after(V.tensor_copy(nt[:, 0:w], nt_i[:, 0:w]))
                    st.after(V.tensor_tensor_scan(tend[:, 0:w], ones[:, 0:1].to_broadcast([P, w]), nt[:, 0:w], 0.0,
                                                  ALU.mult, ALU.add))
                    st.after(V.tensor_tensor(base[:, 0:w], tend[:, 0:w], nt[:, 0:w], ALU.subtract))
                    st.after(V.scalar_tensor_tensor(base[:, 0:w], base[:, 0:w], float(P), before_p[:, 0:w], ALU.mult, ALU.add))
                    st.after(V.scalar_tensor_tensor(base[:, 0:w], base[:, 0:w], -1.0, cend[:, 0:w], ALU.add, ALU.subtract))
                    st.after(V.tensor_scalar(le[:, 0:w], tend[:, 0:w], part[:, 0:1], None, ALU.is_le))
                    st.after(V.tensor_tensor(le[:, 0:w], le[:, 0:w], weight, ALU.mult))
                    V.reduce_sum(off[:, :], le[:, 0:w], axis=AXX).then_inc(off_ready, 1)
                    st.after(V.tensor_tensor(cu, cu, base[:, 0:w].rearrange("p (b o) -> p b o", o=1).to_broadcast([P, w, n]),
                                             ALU.add))
                    st.after(V.tensor_tensor(cu, cu, oh, ALU.mult))
                    st.after(V.reduce_sum(pos[:, 0:n], cu.rearrange("p b t -> p t b"), axis=AXX))
                    row_of()

                def tabulate():
                    dve.wait_ge(off_row, c + 1)
                    V.tensor_scalar(table_out, table_p, last, None, ALU.min).then_inc(table_ready, 1)
                return count, place, tabulate

            def rank_edges(c):
                def rows():
                    st.after(V.tensor_copy(pos_i[:, :], pos[:, 0:CT]))
                    st.after(V.tensor_scalar(pos_h[:, :], pos_i[:, :], 7, None, ALU.logical_shift_right))
                    st.after(V.tensor_scalar(pos_l[:, :], pos_i[:, :], P - 1, None, ALU.bitwise_and))
                    st.after(V.tensor_scalar(pos_l[:, :], pos_l[:, :], float(ST), None, ALU.mult))
                    st.after(V.tensor_tensor(pos[:, 0:CT], pos_l[:, :], pos_h[:, :], ALU.add))
                    V.tensor_tensor(rows_i[:, ds(c * CT, CT)], pos[:, 0:CT], chunk_base[:, ds(c, 1)].to_broadcast([P, CT]),
                                    ALU.add).then_inc(rows_ready, 1)
                return ranking(blk[:, ds(c * CT, CT)], CT, NB, c, rows, slot_w[:, :], float(4 * BANK),
                               table[0:1, ds(c, 1), :].rearrange("a o t -> a (o t)"))

            st.after(V.tensor_scalar(chunk_base[:, :], iota[:, 0:CHUNKS], float(P * ST), None, ALU.mult))
            n0 = st.n
            for part_of_it in rank_edges(0):
                part_of_it()
            steps = st.n - n0
            for part_of_it in rank_edges(1):
                part_of_it()

            dve.wait_ge(rw_summed, 1)
            for k in range(2):
                V.scalar_tensor_tensor(rwc[:, k, :], rw_sum, -1.0 / CH, rw_sb[:, k, :], ALU.mult, ALU.add).then_inc(rwc_ready, 1)

            dve.wait_ge(x_in, 16)
            def block_stats(b, r):
                settled(dve)
                V.bn_stats(stats[:, r, :], xs[:, ds(b, 1), :].rearrange("p o c -> p (o c)")).then_inc(dve_step, 1)

            def group_stats(g):
                st.n = st.n + PRE
                dve.wait_ge(dve_step, st.n)
                settled(dve)
                for r in range(PRE):
                    V.bn_aggr(mv5[:, r, :], stats[:, r, :]).then_inc(dve_step, 1)
                st.n = st.n + PRE
                dve.wait_ge(dve_step, st.n)
                V.tensor_copy(mv[:, ds(PRE * g, PRE), :], mv5[:, :, :]).then_inc(var_ready, 1)
            with dve.Fori(0, NG) as g:
                def all_stats(g):
                    for r in range(PRE):
                        block_stats(PRE * g + r, r)
                    group_stats(g)
                st.loop(g, 0, NG, 2 * PRE, all_stats)
            dve.wait_ge(std_ready, 1)
            st.after(V.tensor_scalar(gain[:, :], rstd[:, :], 1.0, None, ALU.add))
            st.after(V.reciprocal(rstd[:, :], rstd[:, :]))
            dve.wait_ge(wur_done, 1)
            dve.wait_ge(mw_in, 16 * 6)
            dve.wait_ge(consts, 4)
            V.tensor_copy(wu_sb[:, CH:CH + EXPERTS], wur_p).then_inc(wur_ready, 1)
            V.tensor_copy(wu_sb[AD:AD + EXPERTS, CH + EXPERTS:CH + 2 * EXPERTS], ident[AD:AD + EXPERTS, AD:AD + EXPERTS]
                          ).then_inc(wur_ready, 1)

            def normed(to, b, ready):
                xb = xs[:, ds(b, 1), :].rearrange("p o c -> p (o c)")
                V.tensor_scalar(to, xb, mv[:, ds(b, 1), 0], rstd[:, ds(b, 1)], ALU.subtract, ALU.mult).then_inc(ready, 1)
            with dve.Fori(0, NG) as g:
                def norm(g):
                    dve.wait_ge(tr_done, 1 + PRE * g)
                    for r in range(PRE):
                        normed(nrm[:, r, :], PRE * g + r, xn_ready)
                    dve.wait_ge(xn_ready, PRE * g + PRE)
                    group = xs[:, ds(PRE * g, PRE), :]
                    st.after(V.tensor_tensor(group, group, nrm[:, :, :], ALU.add))
                st.loop(g, 0, NG, 1, norm)
            for part_of_it in rank_edges(2):
                part_of_it()

            def take_piece(c, i, alone=True):
                n = PAIRS * c + i
                rows, feats, into = piece_parts(i)
                piece_is_in(dve, c, i)
                if alone:
                    V.tensor_copy(into[0], rows[:, :, 0:AD + 1]).then_inc(part_ready[0], 1)
                    dve.wait_ge(part_ready[0], n + 1)
                else:
                    dve.wait_ge(last_part[0], i + 1)
                V.tensor_tensor(feats, feats, into[0][:, :, 0:AD], ALU.subtract).then_inc(left_ready, 1)
                if alone:
                    dve.wait_ge(left_ready, n + 1)
                    V.tensor_copy(into[1], feats).then_inc(part_ready[1], 1)
                for r in range(GRPS):
                    V.tensor_tensor(node_oh[:, i % 2, r, :].rearrange("p (j n) -> p j n", n=P),
                                    rows[:, r * GRP:(r + 1) * GRP, ROW - 1:ROW].to_broadcast([P, GRP, P]),
                                    iota[:, :].rearrange("p (o n) -> p o n", o=1).to_broadcast([P, GRP, P]),
                                    ALU.is_equal).then_inc(oh_ready[r], 1)
                if alone:
                    dve.wait_ge(part_ready[1], n + 1)
                else:
                    dve.wait_ge(last_part[1], i + 1)
                V.tensor_tensor(into[2], feats, into[1], ALU.subtract).then_inc(part_ready[2], 1)
            with dve.Fori(1, CHUNKS - 2) as s:
                def mid(s):
                    ranks = rank_edges(s + 2)
                    for i in range(PAIRS):
                        take_piece(s - 1, i)
                        if i < len(ranks):
                            ranks[i]()
                st.loop(s, 1, CHUNKS - 2, steps, mid)
            for c in range(CHUNKS - 3, CHUNKS):
                for i in range(PAIRS):
                    take_piece(c, i, alone=c < CHUNKS - 1)

            for r in range(GRPS):
                dve.wait_ge(oh_used[r], 2 + PAIRS * CHUNKS)
            dve.wait_ge(nf_ready, 1 + NB)
            for k in range(4):
                a, z = k * PER_BANK, min(NB, (k + 1) * PER_BANK)
                sl = slots[:, k, 0:(z - a) * SLOT].rearrange("p (b f) -> p b f", f=SLOT)
                st.after(V.tensor_scalar(rcount[:, a:z], sl[:, :, AD], 1.0, None, ALU.max))
            st.after(V.reciprocal(rcount[:, :], rcount[:, :]))
            for k in range(4):
                a, z = k * PER_BANK, min(NB, (k + 1) * PER_BANK)
                sl = slots[:, k, 0:(z - a) * SLOT].rearrange("p (b f) -> p b f", f=SLOT)
                V.tensor_tensor(tmean[:, a * AD:z * AD].rearrange("p (b f) -> p b f", f=AD), sl[:, :, 0:AD],
                                rcount[:, a:z].rearrange("p (b o) -> p b o", o=1).to_broadcast([P, z - a, AD]),
                                ALU.mult).then_inc(mean_ready, 1)

            def add_group(g):
                for r in range(PRE):
                    b = PRE * g + r
                    xb = xs[:, ds(b, 1), :].rearrange("p o c -> p (o c)")
                    dve.wait_ge(up_done, 1 + b + 1)
                    lg = parts[:, ds(b, 1), :].rearrange("p o e -> p (o e)")
                    V.tensor_tensor(xb, xb, up_p[r][:, 0:CH], ALU.add).then_inc(x1_ready, 1)
                    V.tensor_copy(lg, up_p[r][:, CH:CH + 2 * EXPERTS]).then_inc(lg_ready, 1)
                    dve.wait_ge(x1_ready, 1 + b + 1)
                    block_stats(b, r)
                group_stats(g)

            def rstd_group(g):
                blocks = ds(PRE * g, PRE)
                dve.wait_ge(std_ready, 1 + g + 1)
                V.reciprocal(rstd[:, blocks], rstd[:, blocks]).then_inc(rstd_ready, 1)

            def route_group(g):
                blocks, lg, by_block, by_expert = group_logits(g)
                dve.wait_ge(lg_whole, g + 1)
                settled(dve)
                st.after(V.reduce_max(top[:, blocks], lg, axis=AXX))
                st.after(V.tensor_tensor(lg, lg, by_block(top), ALU.is_equal))
                st.after(V.tensor_tensor(lg, lg, by_expert(from_last), ALU.mult))
                settled(dve)
                st.after(V.reduce_max(top[:, blocks], lg, axis=AXX))
                st.after(V.tensor_scalar(blk[:, blocks], top[:, blocks], -1.0, float(EXPERTS), ALU.mult, ALU.add))
            ROUTE_STEPS = 5
            add_group(0)
            with dve.Fori(1, NG - 1) as g:
                def step(g):
                    rstd_group(g - 1)
                    add_group(g)
                    route_group(g - 1)
                st.loop(g, 1, NG - 1, 2 * PRE + ROUTE_STEPS, step)
            rstd_group(NG - 2)
            add_group(NG - 1)
            rstd_group(NG - 1)
            route_group(NG - 2)
            route_group(NG - 1)

            def tokens_of_tiles():
                st.after(V.tensor_copy(pos_i[:, 0:NB], pos[:, 0:NB]))
                st.after(V.tensor_scalar(pos_h[:, 0:NB], pos_i[:, 0:NB], 7, None, ALU.logical_shift_right))
                st.after(V.tensor_scalar(pos_l[:, 0:NB], pos_i[:, 0:NB], P - 1, None, ALU.bitwise_and))
                in_tile = lambda a: a[:, 0:NB].rearrange("p (b o) -> p b o", o=1)
                first, second = lefts[:, :, 0, :], lefts[:, :, 1, :]
                st.after(V.tensor_tensor(first, in_tile(pos_h).to_broadcast([P, NB, XT]),
                                         iota[:, 0:XT].rearrange("p (o t) -> p o t", o=1).to_broadcast([P, NB, XT]), ALU.is_equal))
                V.tensor_scalar(second, first, parts_left[:, 0:1], None, ALU.mult).then_inc(oh_built, 1)
                dve.wait_ge(oh_built, 1)
                V.tensor_tensor(first, first, in_tile(blocks_left).to_broadcast([P, NB, XT]), ALU.mult).then_inc(oh_built, 1)
                for g in range(NG):
                    a = g * PRE
                    V.tensor_tensor(place_oh[:, a * P:(a + PRE) * P].rearrange("p (b j) -> p b j", j=P),
                                    pos_l[:, a:a + PRE].rearrange("p (b o) -> p b o", o=1).to_broadcast([P, PRE, P]),
                                    iota[:, :].rearrange("p (o j) -> p o j", o=1).to_broadcast([P, PRE, P]),
                                    ALU.is_equal).then_inc(oh_built, 1)
            for part_of_it in ranking(blk[:, 0:NB], NB, EXPERTS, CHUNKS, tokens_of_tiles, ones[:, 0:EXPERTS], float(EXPERTS - 1),
                                      table[0:1, CHUNKS, :]):
                part_of_it()
            dve.wait_ge(perm_summed, 1)
            st.after(V.tensor_scalar(perm_f[:, :], perm_p[:, 0:XT], -float(P), float(NO_NODE), ALU.mult, ALU.add))
            V.tensor_tensor(perm[:, :], perm_f[:, :], perm_p[:, XT:2 * XT], ALU.subtract).then_inc(perm_ready, 1)

            dve.wait_ge(late_in, 16 * LATE)
            dve.wait_ge(tr_done, 1 + NB)
            dve.wait_ge(table_ready, CHUNKS + 1)
            def tile_expert(t):
                fixed = isinstance(t, int)
                first = max(0, t - 2) if fixed else t - 2
                n = min(4, XT - first) if fixed else 4
                _, e = nc.values_load_multi_w_load_instructions(
                    table[0:1, CHUNKS, ds(first, n)], engines=[mybir.EngineType.DVE], min_val=0, max_val=EXPERTS - 1,
                    skip_runtime_bounds_check_because="clamped to the last expert")
                lead = t - first if fixed else 2
                return {k - lead: v for k, v in enumerate(e)}

            def step(t, r, expert):
                fixed = isinstance(t, int)
                if not (fixed and t >= XT):
                    dve.wait_ge(tok_loaded[r], 2 * (t - r) + 16)
                    if not (fixed and t < 4):
                        dve.wait_ge(tok_tr, t - 3)
                    V.tensor_scalar(nrm[:, r % 4, :], tok_in[:, r, 0:CH], tok_in[:, r, CH:CH + 1], tok_in[:, r, CH + 1:CH + 2],
                                    ALU.subtract, ALU.mult).then_inc(tok_normed, 1)
                j = t - 2
                if not (fixed and (j < 0 or j >= XT)):
                    dve.wait_ge(hid_done, j + 1)
                    if not (fixed and j < 2):
                        dve.wait_ge(ht_done, j - 1)
                    V.tensor_tensor(hid[:, r % 2, :], hid_p[r % 2], b1_sb[:, ds(expert[r % 4 - 2] * AD, AD)], ALU.add
                                    ).then_inc(hid_ready, 1)
                j, r = t - 4, (r - 4) % RING
                if not (fixed and (j < 0 or j >= XT)):
                    dve.wait_ge(o_done, j + 1)
                    if not (fixed and j < RING):
                        dve.wait_ge(stored[r], 2 * (j - r))
                    V.scalar_tensor_tensor(tok_res[:, r, 0:CH], res_p[r % 2], 0.0, tok_in[:, r, 0:CH], ALU.max, ALU.add
                                           ).then_inc(o_ready, 1)
            expert_steps(dve, step, tile_expert, 4)

        @block.tensor
        def _(pe):
            T = nc.tensor

            def rank_sums(c, w):
                pe.wait_ge(cnt_ready, c + 1)
                T.matmul(before_p[:, 0:w], before[:, :], cnt[:, 0:w], start=True, stop=True)
                T.matmul(total_p[:, 0:w], ones[:, :], cnt[:, 0:w], start=True, stop=True).then_inc(cnt_sum, 1)

            def rank_row(c):
                pe.wait_ge(off_ready, c + 1)
                T.matmul(table_p, off[:, 0:1], ident[:, :], start=True, stop=True).then_inc(off_row, 1)

            def time_features(q, between=lambda h: None):
                for h in range(2):
                    pe.wait_ge(attr_in[h], 32 * (q + 1))
                    pe.wait_ge(ring_ready[h], 1 + 3 * q)
                    for a in range(2):
                        T.matmul(tf_p[h][:, a * 3 * AD:(a + 1) * 3 * AD], attr_sb[:, h, a * P:(a + 1) * P], wt_sb[:, :],
                                 start=True, stop=True)
                    last = T.matmul(tf_p[h][:, 6 * AD:7 * AD], attr_sb[0:ED + 1, h, 2 * P:3 * P], wt1_sb[:, :],
                                    start=True, stop=True)
                    last.then_inc(tf_done[h], 1)
                    between(h)

            def reduce_piece(c, i):
                pe.wait_ge(part_ready[2], 2 + PAIRS * c + i + 1)
                for r in range(GRPS):
                    t0 = i * PIECE + r * GRP
                    _, place = nc.values_load_multi_w_load_instructions(
                        table[0:1, ds(c, 1), t0:t0 + GRP].rearrange("a o t -> a (o t)"), engines=[mybir.EngineType.PE],
                        min_val=0, max_val=3 * BANK + 4 * SLOT,
                        skip_runtime_bounds_check_because="a sum of slot widths up to the spare slot")
                    pe.wait_ge(oh_ready[r], c * PAIRS + i + 1)
                    for j in range(GRP):
                        for part, w in zip(split, (AD + 1, AD, AD)):
                            a = (r * GRP + j) * w
                            last = T.matmul(sums[:, ds(place[j], w)], node_oh[:, i % 2, r, j * P:(j + 1) * P],
                                            part[:, i % 2, a:a + w], start=False, stop=True, skip_group_check=True)
                    last.then_inc(oh_used[r], 1)

            pe.wait_ge(consts, 4)
            pe.wait_ge(ones_set, 1)
            rank_sums(0, NB)
            pe.wait_ge(gw_in, 16 * 8)
            pe.wait_ge(rows_set, 5)
            time_features(0)
            rank_row(0)
            rank_sums(1, NB)
            rank_row(1)
            time_features(1)
            pe.wait_ge(mw_in, 16 * 6)

            def prepare_group(g):
                def transposed(r):
                    b = g * PRE + r
                    pe.wait_ge(xn_ready, b + 1)
                    pe.wait_ge(tr_copied, 1 + b)
                    for k in range(2):
                        last = T.transpose(trp[:, k * P:(k + 1) * P], nrm[:, r, k * P:(k + 1) * P], ident[:, :])
                    last.then_inc(tr_done, 1)

                def features(r):
                    b = g * PRE + r
                    pe.wait_ge(tr_copied, 1 + b + 1)
                    pe.wait_ge(nf_ready, 1 + b)
                    pe.wait_ge(lg_kept, 1 + b)
                    for k in range(2):
                        last = T.matmul(nf_p, wd_sb[:, k, :], xT[:, r % 3, k * P:(k + 1) * P], start=(k == 0), stop=(k == 1))
                    last.then_inc(nf_done, 1)
                def half(h):
                    if h == 0:
                        transposed(0)
                    for r in PRE_HALVES[h]:
                        if r + 1 < PRE:
                            transposed(r + 1)
                        features(r)
                return half
            for k in range(2):
                last = T.matmul(rw_sum, ones[:, :], rw_sb[:, k, :], start=(k == 0), stop=(k == 1))
            last.then_inc(rw_summed, 1)
            time_features(2)
            pe.wait_ge(rwc_ready, 2)
            for k in range(2):
                last = T.matmul(wur_p, wub_sb[:, k, :], rwc[:, k, :], start=(k == 0), stop=(k == 1))
            last.then_inc(wur_done, 1)
            with pe.Fori(0, PRE - 1) as g:
                time_features(g + 3, between=prepare_group(g))
            last_group = prepare_group(PRE - 1)
            last_group(0)
            rank_sums(2, NB)
            last_group(1)
            rank_row(2)
            time_features(PAIRS + PRE - 2)
            pe.wait_ge(nf_ready, 1 + NB)
            pe.wait_ge(lg_kept, 1 + NB)
            pe.wait_ge(wur_ready, 2)
            for k in range(4):
                T.matmul(slots[:, k, :], zrow[:, 0:P], zrow[:, :], start=True, stop=True)

            def stage(s, ranks=True):
                for i in range(PAIRS):
                    if due(s, i):
                        time_features(s * PAIRS + i + AHEAD)
                    if i == 0:
                        pe.wait_ge(table_ready, s)
                    if i == 2 and ranks:
                        rank_row(s + 2)
                    reduce_piece(s - 1, i)
                    if i == 0 and ranks:
                        rank_sums(s + 2, NB)

            stage(1)
            with pe.Fori(2, CHUNKS - 2) as s:
                stage(s)
            stage(CHUNKS - 2, ranks=False)
            stage(CHUNKS - 1, ranks=False)
            pe.wait_ge(table_ready, CHUNKS)
            for i in range(PAIRS):
                reduce_piece(CHUNKS - 1, i)

            pe.wait_ge(late_in, 16 * LATE)
            def mean_rows(g):
                pe.wait_ge(mean_ready, min(-(-PRE * (g + 1) // PER_BANK), 4))
                if g:
                    pe.wait_ge(mt_copied, 2 * g)
                if g > 1:
                    pe.wait_ge(x1_ready, 1 + PRE * (g - 1))
                    pe.wait_ge(lg_ready, 1 + PRE * (g - 1))
                for r in range(PRE):
                    to = tf_p[r // 4][0:AD, r % 4 * P:(r % 4 + 1) * P]
                    a = (PRE * g + r) * AD
                    last = T.transpose(to, tmean[:, a:a + AD], ident[:, :])
                last.then_inc(mt_done, 1)

            def fuse(g):
                pe.wait_ge(mt_copied, 2 * g + 2)
                pe.wait_ge(fu_ready, 1 + 3 * g)
                for k in range(2):
                    last = T.matmul(fused_p[k], wf_sb[:, :], combT[:, ds(g * (PRE * P) + k * HALF, HALF)], start=True, stop=True)
                last.then_inc(fu_done, 1)

            def up(g):
                pe.wait_ge(mean_ready, 4)
                pe.wait_ge(fu_ready, 1 + 3 * g + 3)
                for r in range(PRE):
                    if g:
                        pe.wait_ge(x1_ready, 1 + PRE * (g - 1) + r + 1)
                        pe.wait_ge(lg_ready, 1 + PRE * (g - 1) + r + 1)
                    if r == PRE - 1 and g < NG - 1:
                        pe.wait_ge(mt_copied, 2 * (g + 2))
                    T.matmul(up_p[r], fT[:, r * P:(r + 1) * P], wu_sb[:, :], start=True, stop=True).then_inc(up_done, 1)
            mean_rows(0)
            for g in range(NG - 1):
                fuse(g)
                mean_rows(g + 1)
                up(g)
            fuse(NG - 1)
            up(NG - 1)
            pe.wait_ge(x1_ready, 1 + NB)
            pe.wait_ge(lg_ready, 1 + NB)

            rank_sums(CHUNKS, EXPERTS)
            rank_row(CHUNKS)
            for b in range(NB):
                if b % PRE == 0:
                    pe.wait_ge(oh_built, 2 + b // PRE + 1)
                last = T.matmul(perm_p, place_oh[:, b * P:(b + 1) * P], lefts[:, b, :, :].rearrange("p k t -> p (k t)"),
                                start=(b == 0), stop=(b == NB - 1))
            last.then_inc(perm_summed, 1)
            pe.wait_ge(perm_ready, 1)
            pe.wait_ge(table_ready, CHUNKS + 1)

            def tile_experts(t):
                fixed = isinstance(t, int)
                first = max(0, t - 3) if fixed else t - 3
                n = min(6, XT - first) if fixed and t >= XT else 6
                _, e = nc.values_load_multi_w_load_instructions(
                    table[0:1, CHUNKS, ds(first, n)], engines=[mybir.EngineType.PE], min_val=0, max_val=EXPERTS - 1,
                    skip_runtime_bounds_check_because="clamped to the last expert")
                lead = t - first if fixed else 3
                return {k - lead: v for k, v in enumerate(e)}

            def step(t, r, expert):
                fixed = isinstance(t, int)
                h, o = r % 2, (r + 1) % 2
                if not (fixed and t >= XT):
                    pe.wait_ge(tok_normed, t + 1)
                    if not (fixed and t < 2):
                        pe.wait_ge(tok_trc, t - 1)
                    for k in range(2):
                        last = T.transpose(tok_p[h][:, k * P:(k + 1) * P], nrm[:, r % 4, k * P:(k + 1) * P], ident[:, :])
                    last.then_inc(tok_tr, 1)
                j = t - 1
                if not (fixed and (j < 0 or j >= XT)):
                    e = expert[r % 4 - 1]
                    pe.wait_ge(tok_trc, j + 1)
                    if not (fixed and j < 2):
                        pe.wait_ge(hid_ready, j - 1)
                    for k in range(2):
                        last = T.matmul(hid_p[o], xT[:, o, k * P:(k + 1) * P], w1_sb[:, ds(e * (2 * AD) + k * AD, AD)],
                                        start=(k == 0), stop=(k == 1))
                    last.then_inc(hid_done, 1)
                j = t - 2
                if not (fixed and (j < 0 or j >= XT)):
                    pe.wait_ge(hid_ready, j + 1)
                    if not (fixed and j < 2):
                        pe.wait_ge(ht_ready, j - 1)
                    settled(pe)
                    T.transpose(hT_p[h], hid[:, h, :], ident[:, :]).then_inc(ht_done, 1)
                j = t - 3
                if not (fixed and (j < 0 or j >= XT)):
                    e = expert[r % 4 - 3]
                    pe.wait_ge(ht_ready, j + 1)
                    if not (fixed and j < 2):
                        pe.wait_ge(o_ready, j - 1)
                    T.matmul(res_p[o], hT[:, o * P:(o + 1) * P], w2_sb[:, ds(e * CH, CH)], start=True, stop=True
                             ).then_inc(o_done, 1)
            expert_steps(pe, step, tile_experts)


_ARGS = ["x", "src", "attr_3", "attr_1", "wd_t", "bd", "wt_t", "bt", "wf_t", "bf", "wu_t", "bu", "wu_b", "rw_t", "rb", "w1", "b1", "w2", "b2"]


def kernel(**inputs):
    import concourse.bacc as bacc
    from concourse.bass_utils import run_bass_kernel_spmd

    a = {k: np.ascontiguousarray(v) for k, v in inputs.items()}
    c = np.ascontiguousarray
    x = np.zeros((NB * P, CH), a["x"].dtype)
    x[:NODES] = a["x"]
    src = np.full((ET * P,), NB * P - 1, a["src"].dtype)
    src[:EDGES] = a["src"]
    attr = np.zeros((ET * P, ED), a["edge_attr_32"].dtype)
    attr[:EDGES] = a["edge_attr_32"]
    attr = attr.reshape(P, ET // BATCH, BATCH, ED).transpose(1, 2, 3, 0)
    attr_3 = c(attr[:, 0:6].reshape(ET // BATCH, 2, 3 * ED, P).transpose(2, 0, 1, 3)).reshape(3 * ED, ET // BATCH * 2 * P)
    attr_1 = c(attr[:, 6].transpose(1, 0, 2)).reshape(ED, ET // BATCH * P)
    arrays = {
        "x": x, "src": src,
        "attr_3": attr_3, "attr_1": attr_1,
        "wd_t": c(a["L0_gnn_W_down"].T), "bd": a["L0_gnn_b_down"].reshape(AD, 1),
        "wt_t": c(a["L0_gnn_W_time"].T), "bt": a["L0_gnn_b_time"].reshape(1, AD),
        "wf_t": c(a["L0_gnn_W_fusion"].T), "bf": a["L0_gnn_b_fusion"].reshape(AD, 1),
        "wu_t": c(a["L0_gnn_W_up"].T), "bu": a["L0_gnn_b_up"].reshape(1, CH),
        "wu_b": c(np.concatenate([a["L0_gnn_W_up"], np.zeros((CH, EXPERTS), a["L0_gnn_W_up"].dtype),
                                   a["L0_gnn_b_up"][:, None]], axis=1)),
        "rw_t": c(a["L0_ffn_router_w"].T), "rb": a["L0_ffn_router_b"].reshape(1, EXPERTS),
        "w1": c(a["L0_ffn_W1"].reshape(EXPERTS, 2, P, AD).transpose(2, 0, 1, 3)).reshape(P, EXPERTS * 2 * AD),
        "b1": a["L0_ffn_b1"].reshape(1, EXPERTS * AD),
        "w2": c(a["L0_ffn_W2"].transpose(1, 0, 2)).reshape(AD, EXPERTS * CH), "b2": a["L0_ffn_b2"].reshape(1, EXPERTS * CH),
    }
    nc = bacc.Bacc("TRN2", target_bir_lowering=False, num_devices=1)
    maps, aps = {}, []
    for name in _ARGS:
        maps[f"{name}_dram"] = arrays[name]
        aps.append(nc.dram_tensor(f"{name}_dram", arrays[name].shape, mybir.dt.from_np(arrays[name].dtype),
                                  kind="ExternalInput").ap())
    out = nc.dram_tensor("out_dram", (NODES, CH), f32, kind="ExternalOutput").ap()
    program(nc, *aps, out)
    r = run_bass_kernel_spmd(nc, [maps], core_ids=[0])
    return r.results[0]["out_dram"]
```
